# Optimizing a Trainium2 kernel written in Bass

```python
import numpy as np
import jax
import jax.numpy as jnp

def _softmax(x, axis=-1):
    return jax.nn.softmax(x, axis=axis)

def _gelu(x):
    return jax.nn.gelu(x, approximate=True)

def _silu(x):
    return jax.nn.silu(x)

def _sigmoid(x):
    return jax.nn.sigmoid(x)

def _layernorm(x, axis=-1, eps=1e-05):
    m = jnp.mean(x, axis=axis, keepdims=True)
    v = jnp.var(x, axis=axis, keepdims=True)
    return (x - m) / jnp.sqrt(v + eps)

def _scatter_add(tgt, idx, src, axis=0):
    return tgt.at[idx].add(src)

def _segment_sum(src, seg, n):
    return jax.ops.segment_sum(src, seg, n)
kernel_name = 'mk_gnn_ffn_d1_gnn_r8_c7de70'

def setup_inputs(seed: int=0):
    np.random.seed(seed)
    _w = jnp.asarray

    def _rec_inputs():
        import jax
        import jax.numpy as jnp
        _gk = jax.random.key(seed)
        x = -0.0003713 + 1 * jax.random.normal(jax.random.fold_in(_gk, 1), (6250, 256), jnp.float32)
        src = jax.random.randint(jax.random.fold_in(_gk, 2), (200000,), 0, 6250, jnp.int32)
        dst = jax.random.randint(jax.random.fold_in(_gk, 3), (200000,), 0, 6250, jnp.int32)
        _o = jnp.argsort(dst, stable=True)
        src = src[_o]
        dst = dst[_o]
        edge_type_8 = jax.random.randint(jax.random.fold_in(_gk, 12), (200000,), 0, 8, jnp.int32)
        return (x, src, dst, edge_type_8)
    x, src, dst, edge_type_8 = _rec_inputs()

    def _L0_gnn_setup():
        import jax, jax.numpy as jnp
        import numpy as np
        N_NODES = 6250
        N_EDGES = 37500
        N_REL = 8
        D = 256
        N_LAYERS = 3

        def _rgcn_layer(x, W, root, bias, src, dst, seg):
            agg = jax.ops.segment_sum(x[src], seg, num_segments=N_REL * N_NODES)
            agg = agg.reshape(N_REL, N_NODES, -1)
            return jnp.einsum('rnd,rde->ne', agg, W) + x @ root + bias
        key = jax.random.key(seed)
        k1, k2, k3, k4, k5 = jax.random.split(key, 5)
        x = jax.random.normal(k1, (N_NODES, D), dtype=jnp.float32)
        scale = 1.0 / np.sqrt(D)
        weights = jax.random.normal(k2, (N_LAYERS, N_REL, D, D), dtype=jnp.float32) * scale
        roots = jax.random.normal(k3, (N_LAYERS, D, D), dtype=jnp.float32) * scale
        biases = jnp.zeros((N_LAYERS, D), dtype=jnp.float32)
        edge_index = jax.random.randint(k4, (2, N_EDGES), 0, N_NODES, dtype=jnp.int64)
        edge_type = jax.random.randint(k5, (N_EDGES,), 0, N_REL, dtype=jnp.int64)
        return {'x': x, 'weights': weights, 'roots': roots, 'biases': biases, 'edge_index': edge_index, 'edge_type': edge_type}
    _L0_gnn_all = _L0_gnn_setup()
    _L0_gnn_in = {k: v for k, v in _L0_gnn_all.items() if k in ('weights', 'roots', 'biases')}
    del _L0_gnn_all

    def _L0_ffn_setup():
        import jax, jax.numpy as jnp
        import numpy as np
        NUM_EXPERTS = 8
        TOP_K = 2
        B, S, D = (8, 1024, 256)

        def _moe(tokens, router_w, w1, b1, w2, b2):
            N = tokens.shape[0]
            E = router_w.shape[0]
            logits = tokens.astype(jnp.float32) @ router_w.astype(jnp.float32).T
            probs = jax.nn.softmax(logits, axis=-1)
            rw, re = jax.lax.top_k(probs, TOP_K)
            if TOP_K > 1:
                rw = rw / jnp.maximum(rw.sum(-1, keepdims=True), 1e-12)
            rw = rw.astype(tokens.dtype)
            combine = jnp.zeros((N, E), tokens.dtype).at[jnp.arange(N)[:, None], re].set(rw)
            out = tokens
            for e in range(E):
                h = jax.nn.gelu(tokens @ w1[e] + b1[e], approximate=False)
                y = h @ w2[e] + b2[e]
                out = out + combine[:, e:e + 1] * y
            return out
        key = jax.random.key(seed)
        ks = jax.random.split(key, 4)
        scale = 1.0 / np.sqrt(D).astype(np.float32)
        return {'input_embeddings': jax.random.normal(ks[0], (B, S, D), jnp.float32), 'router_w': jax.random.normal(ks[1], (NUM_EXPERTS, D), jnp.float32) * scale, 'w1': jax.random.normal(ks[2], (NUM_EXPERTS, D, D), jnp.float32) * scale, 'b1': jnp.zeros((NUM_EXPERTS, D), jnp.float32), 'w2': jax.random.normal(ks[3], (NUM_EXPERTS, D, D), jnp.float32) * scale, 'b2': jnp.zeros((NUM_EXPERTS, D), jnp.float32)}
    _L0_ffn_all = _L0_ffn_setup()
    _L0_ffn_in = {k: v for k, v in _L0_ffn_all.items() if k in ('router_w', 'w1', 'b1', 'w2', 'b2')}
    del _L0_ffn_all
    return {'x': x, 'src': src, 'dst': dst, 'edge_type_8': edge_type_8, 'L0_gnn_weights': _L0_gnn_in['weights'], 'L0_gnn_roots': _L0_gnn_in['roots'], 'L0_gnn_biases': _L0_gnn_in['biases'], 'L0_ffn_router_w': _L0_ffn_in['router_w'], 'L0_ffn_w1': _L0_ffn_in['w1'], 'L0_ffn_b1': _L0_ffn_in['b1'], 'L0_ffn_w2': _L0_ffn_in['w2'], 'L0_ffn_b2': _L0_ffn_in['b2']}

def reference(x, src, dst, edge_type_8, L0_gnn_weights, L0_gnn_roots, L0_gnn_biases, L0_ffn_router_w, L0_ffn_w1, L0_ffn_b1, L0_ffn_w2, L0_ffn_b2):
    import jax
    import jax.numpy as jnp

    def _L0_gnn_ref(x, weights, roots, biases, edge_index, edge_type):
        import jax, jax.numpy as jnp
        import numpy as np
        N_NODES = 6250
        N_EDGES = 37500
        N_REL = 8
        D = 256
        N_LAYERS = 3

        def _rgcn_layer(x, W, root, bias, src, dst, seg):
            agg = jax.ops.segment_sum(x[src], seg, num_segments=N_REL * N_NODES)
            agg = agg.reshape(N_REL, N_NODES, -1)
            return jnp.einsum('rnd,rde->ne', agg, W) + x @ root + bias
        src, dst = (edge_index[0], edge_index[1])
        seg = edge_type * N_NODES + dst
        h = x
        for l in range(N_LAYERS - 1):
            h = jax.nn.relu(_rgcn_layer(h, weights[l], roots[l], biases[l], src, dst, seg))
        h = jax.nn.sigmoid(_rgcn_layer(h, weights[-1], roots[-1], biases[-1], src, dst, seg))
        return h

    def _L0_ffn_ref(input_embeddings, router_w, w1, b1, w2, b2):
        import jax, jax.numpy as jnp
        import numpy as np
        NUM_EXPERTS = 8
        TOP_K = 2
        B, S, D = (8, 1024, 256)

        def _moe(tokens, router_w, w1, b1, w2, b2):
            N = tokens.shape[0]
            E = router_w.shape[0]
            logits = tokens.astype(jnp.float32) @ router_w.astype(jnp.float32).T
            probs = jax.nn.softmax(logits, axis=-1)
            rw, re = jax.lax.top_k(probs, TOP_K)
            if TOP_K > 1:
                rw = rw / jnp.maximum(rw.sum(-1, keepdims=True), 1e-12)
            rw = rw.astype(tokens.dtype)
            combine = jnp.zeros((N, E), tokens.dtype).at[jnp.arange(N)[:, None], re].set(rw)
            out = tokens
            for e in range(E):
                h = jax.nn.gelu(tokens @ w1[e] + b1[e], approximate=False)
                y = h @ w2[e] + b2[e]
                out = out + combine[:, e:e + 1] * y
            return out
        b, s, d = input_embeddings.shape
        tokens = input_embeddings.reshape(b * s, d)
        return _moe(tokens, router_w, w1, b1, w2, b2).reshape(b, s, d)
    edge_index = jnp.stack([src, dst])
    x = x + _L0_gnn_ref(_layernorm(x, axis=-1), L0_gnn_weights, L0_gnn_roots, L0_gnn_biases, edge_index, edge_type_8)
    x = x + _L0_ffn_ref(_layernorm(x, axis=-1)[None], L0_ffn_router_w, L0_ffn_w1, L0_ffn_b1, L0_ffn_w2, L0_ffn_b2)[0]
    return x

_drawn_inputs = setup_inputs


def setup_inputs(seed=0):
    import zlib

    import numpy as np

    out = dict(_drawn_inputs(seed))
    spreads = {'L0_gnn_biases': (0.0, 0.1), 'L0_ffn_b1': (0.0, 0.354), 'L0_ffn_b2': (0.0, 0.1)}
    factors = {}
    for name, (base, spread) in spreads.items():
        noise = np.random.default_rng([zlib.crc32(name.encode()), seed]).standard_normal(out[name].shape)
        drawn = base * np.exp(spread * noise) if base else spread * noise
        out[name] = jnp.asarray(drawn.astype(out[name].dtype))
    for name, factor in factors.items():
        out[name] = (out[name] * factor).astype(out[name].dtype)
    return out
```

```python
from contextlib import ExitStack

import concourse.bass as bass
from concourse import mybir

ALU = mybir.AluOpType
ACT = mybir.ActivationFunctionType
AX = mybir.AxisListType
F32 = mybir.dt.float32
BF16 = mybir.dt.bfloat16
I32 = mybir.dt.int32
U32 = mybir.dt.uint32

P = 128
BATCH = 9
RING = 3
SLOTS = BATCH * RING
PARTS = 3
EPS = 1e-5


def round_up(n, m):
    return -(-n // m) * m


class Chain:

    def __init__(self, eng, sem):
        self.eng, self.sem, self.base, self.k = eng, sem, 0, 0

    def turn(self, base):
        self.base, self.k = base, 0

    def link(self, ins):
        self.k += 1
        ins.then_inc(self.sem, 1)
        self.eng.wait_ge(self.sem, self.base + self.k)


def gnn_moe(nc, x, src, dst, etype, gnn_w, gnn_root, gnn_bias, router_w, w1, b1, w2, b2, out):
    N, D = x.shape
    E = src.shape[0]
    LAYERS, R = gnn_w.shape[0], gnn_w.shape[1]
    EX = w1.shape[0]
    assert D == 256 and R == 8 and LAYERS == 3 and EX == 8
    KD = D // P
    BLOCKS = -(-N // P)
    LAST = N - (BLOCKS - 1) * P
    TILES = -(-E // P)
    STEPS = TILES + BLOCKS - 1
    STAGE = SLOTS
    TILES_P = round_up(TILES, 2 * STAGE)
    STEPS_P = round_up(STEPS, SLOTS)
    CH = -(-max(TILES_P, STEPS_P) // P)
    NQ = STEPS_P // BATCH
    PAD_NODE = BLOCKS * P
    CHUNKS = R * D // 512
    ROW = PARTS * D
    HALF = R // 2 * ROW

    ctx = ExitStack()
    with ctx:
        def sb(name, shape, dt, where=ctx):
            return where.enter_context(nc.sbuf_tensor(name, shape, dt))

        def bank(name):
            return ctx.enter_context(nc.psum_tensor(name, [P, 512], F32))

        def sem(name):
            return ctx.enter_context(nc.semaphore(name))

        tables = [nc.dram_tensor(f"table{i}", [BLOCKS, P, R * ROW], BF16).ap() for i in range(2)]
        onehots = nc.dram_tensor("onehots", [NQ, P, BATCH * P], BF16).ap()
        dst_rows = nc.dram_tensor("dst_rows", [CH * P, P], F32).ap()

        ident = sb("ident", [P, P], F32)
        zeros = sb("zeros", [P, D], BF16)
        gnn_w_sb = sb("gnn_w_sb", [P, KD, R + 1, D], F32)
        bias_sb = sb("bias_sb", [P, LAYERS, D], F32)
        w1_sb = sb("w1_sb", [P, EX, KD, D], F32)
        w2_sb = sb("w2_sb", [P, EX, KD, D], F32)
        b1_rows = sb("b1_rows", [EX * KD, P], F32)
        b1_sb = sb("b1_sb", [P, EX * KD], F32)
        b2_sb = sb("b2_sb", [EX, D], F32)
        rw_rows = sb("rw_rows", [EX, D], F32)
        rw_sb = sb("rw_sb", [P, KD, EX], F32)
        root_sb = sb("root_sb", [P, BLOCKS * D], F32)
        idx_all = sb("idx_all", [P, CH * P], U32)
        stage_idx = [sb(f"stage_idx{i}", [P, STAGE], U32) for i in range(2)]
        hot_ring = sb("hot_ring", [P, SLOTS * P], BF16)
        bounds = sb("bounds", [1, BLOCKS + 1], I32)
        x_sb = sb("x_sb", [P, D], F32)
        h_sb = sb("h_sb", [P, D], F32)
        hT = sb("hT", [P, KD, P], F32)
        residual = [sb(f"residual{i}", [P, 2, D], F32) for i in range(CHUNKS)]
        rows_out = [sb(f"rows_out{i}", [P, R // 2, PARTS, D], BF16) for i in range(2)]
        stats = sb("stats", [P, 6], F32)
        meanvar = sb("meanvar", [P, 2], F32)
        var_eps = sb("var_eps", [P, 1], F32)
        std = sb("std", [P, 1], F32)
        rstd = sb("rstd", [P, 1], F32)
        z_sb = sb("z_sb", [P, D], F32)
        sig_sb = sb("sig_sb", [P, D], F32)
        x1_sb = sb("x1_sb", [P, D], F32)
        acc_sb = sb("acc_sb", [P, D], F32)
        out_sb = sb("out_sb", [P, D], F32)
        hidden_sb = [sb(f"hidden_sb{i}", [P, KD, P], F32) for i in range(2)]
        combT = sb("combT", [EX, P], F32)
        desc8 = sb("desc8", [P, EX], F32)
        lmax = sb("lmax", [P, 1], F32)
        nlmax = sb("nlmax", [P, 1], F32)
        pexp = sb("pexp", [P, EX], F32)
        psum_e = sb("psum_e", [P, 1], F32)
        rpsum = sb("rpsum", [P, 1], F32)
        probs = sb("probs", [P, EX], F32)
        top = sb("top", [P, 2], F32)
        key = sb("key", [P, EX], F32)
        kmax = sb("kmax", [P, 1], F32)
        first = sb("first", [P, EX], F32)
        rest = sb("rest", [P, EX], F32)
        second = sb("second", [P, EX], F32)
        chosen = sb("chosen", [P, EX], F32)
        tsum = sb("tsum", [P, 1], F32)
        rtsum = sb("rtsum", [P, 1], F32)
        comb = sb("comb", [P, EX], F32)

        prep = ExitStack()
        dst_i = sb("dst_i", [P, CH, P], I32, prep)
        src_i = sb("src_i", [P, CH, P], I32, prep)
        typ_i = sb("typ_i", [P, CH, P], I32, prep)
        dst_f = sb("dst_f", [P, CH, P], F32, prep)
        idx_f = sb("idx_f", [P, CH, P], F32, prep)
        dst_sel = sb("dst_sel", [P, CH, P], F32, prep)
        prep.close()
        gathered = sb("gathered", [P, SLOTS * ROW], BF16)
        ones = sb("ones", [P, P], F32)
        loc_all = sb("loc_all", [P, CH * P], BF16)
        iota_i = sb("iota_i", [P, P], I32)
        iota_b = sb("iota_b", [P, P], BF16)
        block_i = sb("block_i", [P, BLOCKS - 1], I32)
        block_f = sb("block_f", [P, BLOCKS - 1], F32)
        thresh = sb("thresh", [P, BLOCKS - 1], F32)
        last_f = sb("last_f", [P, CH], F32)
        below = sb("below", [P, BLOCKS - 1, CH], F32)
        below_n = sb("below_n", [P, BLOCKS - 1], F32)
        start_f = sb("start_f", [P, BLOCKS - 1], F32)
        step_i = sb("step_i", [P, CH], I32)
        step_f = sb("step_f", [P, CH], F32)
        reached = sb("reached", [P, CH, BLOCKS - 1], F32)
        block_of = sb("block_of", [P, CH], F32)
        tile_f = sb("tile_f", [P, CH], F32)
        tile_of = sb("tile_of", [P, CH], U32)
        beyond = sb("beyond", [P, CH], F32)
        shift = sb("shift", [P, CH], F32)

        agg_ps = bank("agg_ps")
        tr_ps = bank("tr_ps")
        y_ps = [bank(f"y_ps{i}") for i in range(CHUNKS)]
        root_ps = bank("root_ps")
        comb_ps = bank("comb_ps")

        padded = sem("padded")
        edges_in = sem("edges_in")
        weights_in = sem("weights_in")
        layer_w_in = sem("layer_w_in")
        consts = sem("consts")
        dve_own = sem("dve_own")
        edges_f = sem("edges_f")
        counted = sem("counted")
        totals = sem("totals")
        bounds_ok = sem("bounds_ok")
        tiles_ok = sem("tiles_ok")
        dst_saved = sem("dst_saved")
        dst_got = sem("dst_got")
        shifted = sem("shifted")
        prep_T = sem("prep_T")
        prep_out = sem("prep_out")
        hot_made = sem("hot_made")
        hot_saved = [sem(f"hot_saved{j}") for j in range(RING)]
        small_T = sem("small_T")
        small_out = sem("small_out")
        x_in = sem("x_in")
        apart = sem("apart")
        var_ready = sem("var_ready")
        std_ready = sem("std_ready")
        h_ready = sem("h_ready")
        transposed = sem("transposed")
        hT_ready = sem("hT_ready")
        y_ready = sem("y_ready")
        part0 = sem("part0")
        resid = sem("resid")
        part1 = sem("part1")
        part2 = sem("part2")
        rows_saved = [sem(f"rows_saved{i}") for i in range(2)]
        root_ready = sem("root_ready")
        root_taken = sem("root_taken")
        staged = sem("staged")
        tile_in = [sem(f"tile_in{j}") for j in range(RING)]
        tile_ready = sem("tile_ready")
        tile_free = sem("tile_free")
        hot_in = [sem(f"hot_in{j}") for j in range(RING)]
        hot_ready = sem("hot_ready")
        hot_free = sem("hot_free")
        agg_done = sem("agg_done")
        z_ready = sem("z_ready")
        sig_ready = sem("sig_ready")
        x1_ready = sem("x1_ready")
        acc_ready = sem("acc_ready")
        logits = sem("logits")
        lmax_ok = sem("lmax_ok")
        pexp_ok = sem("pexp_ok")
        comb_ok = sem("comb_ok")
        combT_ps = sem("combT_ps")
        combT_ok = sem("combT_ok")
        hid_ready = sem("hid_ready")
        gelu_done = sem("gelu_done")
        exp_ready = sem("exp_ready")
        exp_taken = sem("exp_taken")
        b2_ready = sem("b2_ready")
        out_ready = sem("out_ready")
        out_free = sem("out_free")
        out_saved = sem("out_saved")

        def n_of(phase, b):
            return phase * BLOCKS + b

        def relu_rows(t):
            return t.rearrange("b p (r c) -> (b p r) c", r=R)

        hot4 = hot_ring[:, :].rearrange("p (q u e) -> p q u e", q=RING, u=BATCH)

        block = ctx.enter_context(nc.Block())

        @block.sync
        def _(sp):
            full = E // (P * P)
            rows = (E - full * P * P) // P
            tail = E - full * P * P - rows * P
            sp.wait_ge(padded, 3)
            for a, t in ((dst, dst_i), (src, src_i), (etype, typ_i)):
                sp.dma_start(t[:, 0:full, :], a[0:full * P * P].rearrange("(c p e) -> p c e", p=P, e=P)) \
                    .then_inc(edges_in, 16)
                if rows:
                    sp.dma_start(t[0:rows, full, :], a[full * P * P:full * P * P + rows * P]
                                 .rearrange("(p e) -> p e", e=P)).then_inc(edges_in, 16)
                if tail:
                    sp.dma_start(t[rows:rows + 1, full, 0:tail], a[E - tail:E].rearrange("(a e) -> a e", a=1)) \
                        .then_inc(edges_in, 16)

            def layer_weights(layer):
                for k in range(KD):
                    sp.dma_start(gnn_w_sb[:, k, 0:R, :], gnn_w[layer, :, k * P:(k + 1) * P, :]
                                 .rearrange("r p e -> p r e")).then_inc(layer_w_in, 16)
                    sp.dma_start(gnn_w_sb[:, k, R, :], gnn_root[layer, k * P:(k + 1) * P, :]) \
                        .then_inc(layer_w_in, 16)

            layer_weights(0)
            sp.dma_start(x_sb[:, :], x[0:P, :]).then_inc(x_in, 16)
            sp.dma_start(bias_sb[:, :, :], gnn_bias.rearrange("(a l) d -> a l d", a=1).broadcast_to([P, LAYERS, D])) \
                .then_inc(weights_in, 16)
            sp.dma_start(b1_rows[:, :], b1.rearrange("e (k p) -> (e k) p", p=P)).then_inc(weights_in, 16)
            sp.dma_start(rw_rows[:, :], router_w).then_inc(weights_in, 16)
            sp.dma_start(b2_sb[:, :], b2).then_inc(weights_in, 16)
            for k in range(KD):
                sp.dma_start(w1_sb[:, :, k, :], w1[:, k * P:(k + 1) * P, :].rearrange("e p f -> p e f")) \
                    .then_inc(weights_in, 16)
                sp.dma_start(w2_sb[:, :, k, :], w2[:, k * P:(k + 1) * P, :].rearrange("e p f -> p e f")) \
                    .then_inc(weights_in, 16)

            sp.wait_ge(edges_f, 1)
            sp.dma_start(dst_rows.rearrange("(c p) e -> p c e", p=P), dst_f[:, :, :]).then_inc(dst_saved, 16)

            with sp.Fori(1, BLOCKS - 1) as b:
                sp.wait_ge(h_ready, b)
                sp.dma_start(x_sb[:, :], x[bass.ds(b * P, P), :]).then_inc(x_in, 16)
            sp.wait_ge(h_ready, BLOCKS - 1)
            sp.dma_start(x_sb[0:LAST, :], x[(BLOCKS - 1) * P:N, :]).then_inc(x_in, 16)

            for j in range(RING):
                sp.wait_ge(hot_saved[j], 16 * (NQ // RING))
            for layer in range(LAYERS):
                if layer + 1 < LAYERS:
                    sp.wait_ge(root_ready, (layer + 1) * BLOCKS)
                    layer_weights(layer + 1)

                def issue(q, j):
                    sp.wait_ge(hot_free, layer * STEPS_P + BATCH * q + BATCH)
                    src_ap = onehots[q] if isinstance(q, int) else onehots[bass.ds(q, 1)].rearrange("a p e -> (a p) e")
                    sp.dma_start(hot_ring[:, j * BATCH * P:(j + 1) * BATCH * P], src_ap).then_inc(hot_in[j], 16)

                def ready(i, j):
                    sp.wait_ge(hot_in[j], 16 * (layer * (NQ // RING) + i + 1))
                    sp.sem_inc(hot_ready, BATCH)

                issue(0, 0)
                with sp.Fori(0, NQ // RING - 1) as i:
                    for j in range(RING):
                        issue(RING * i + j + 1, (j + 1) % RING)
                        ready(i, j)
                for j in range(1, RING):
                    issue(NQ - RING + j, j)
                    ready(NQ // RING - 1, j - 1)
                ready(NQ // RING - 1, RING - 1)

        @block.gpsimd
        def _(pool):
            pool.memset(ident[:, :], 0.0).then_inc(consts, 1)
            pool.wait_ge(consts, 1)
            pool.affine_select(out=ident[:, :], in_=ident[:, :], compare_op=ALU.not_equal, fill=1.0,
                               base=0, pattern=[[-1, P]], channel_multiplier=1).then_inc(consts, 1)
            pool.iota(iota_i[:, :], pattern=[[1, P]], base=0, channel_multiplier=0).then_inc(consts, 1)
            pool.iota(block_i[:, :], pattern=[[1, BLOCKS - 1]], base=1, channel_multiplier=0).then_inc(consts, 1)
            pool.iota(step_i[:, :], pattern=[[P, CH]], base=0, channel_multiplier=1).then_inc(consts, 1)
            pool.memset(ones[:, :], 1.0).then_inc(consts, 1)
            pool.memset(zeros[:, :], 0.0).then_inc(consts, 1)

            pool.wait_ge(tiles_ok, 1)
            pool.wait_ge(dst_saved, 16)
            for c in range(CH):
                pool.indirect_dma_start(out=dst_sel[:, c, :], out_offset=None, in_=dst_rows,
                                        in_offset=bass.IndirectOffsetOnAxis(ap=tile_of[:, c:c + 1], axis=0)) \
                    .then_inc(dst_got, 16)

            GQ = TILES_P // BATCH
            HALVES = TILES_P // STAGE

            def stage(half, s):
                at = half * STAGE
                cols = idx_all[:, bass.ds(at, STAGE)] if not isinstance(half, int) else idx_all[:, at:at + STAGE]
                pool.tensor_copy(stage_idx[s][:, :], cols).then_inc(staged, 1)

            for layer in range(LAYERS):
                rows_of = relu_rows(tables[layer % 2])

                def landed(turns, j):
                    pool.wait_ge(tile_in[j], 16 * BATCH * (layer * (GQ // RING) + turns))
                    pool.sem_inc(tile_ready, BATCH)

                def half_gathers(half, s, first_half, last_half):
                    pool.wait_ge(staged, layer * HALVES + half + 1)
                    for j in range(RING):
                        pool.wait_ge(tile_free, layer * TILES_P + STAGE * half + BATCH * (j + 1))
                        pool.wait_ge(rows_saved[0], 16 * BLOCKS * (layer + 1))
                        pool.wait_ge(rows_saved[1], 16 * BLOCKS * (layer + 1))
                        pool.sem_inc(apart, 1)
                        for u in range(BATCH):
                            n = j * BATCH + u
                            pool.indirect_dma_start(
                                out=gathered[:, n * ROW:(n + 1) * ROW], out_offset=None, in_=rows_of,
                                in_offset=bass.IndirectOffsetOnAxis(ap=stage_idx[s][:, n:n + 1], axis=0)) \
                                .then_inc(tile_in[j], 16)
                            if u == 2 and not (first_half and j == 0):
                                landed(half if j == 0 else half + 1, (j - 1) % RING)
                            if u == 4 and j == 1 and not last_half:
                                stage(half + 1, 1 - s)

                if layer == 0:
                    pool.wait_ge(prep_out, 2 * CH)
                stage(0, 0)
                half_gathers(0, 0, True, False)
                half_gathers(1, 1, False, False)
                with pool.Fori(1, HALVES // 2 - 1) as i:
                    half_gathers(2 * i, 0, False, False)
                    half_gathers(2 * i + 1, 1, False, False)
                half_gathers(HALVES - 2, 0, False, False)
                half_gathers(HALVES - 1, 1, False, True)
                landed(HALVES, RING - 1)

        @block.scalar
        def _(act):
            Q = NQ // RING

            def post_table(phase, b, first_block=False):
                n = n_of(phase, b)
                act.wait_ge(transposed, n + 1)
                act.activation(hT[:, :, :], tr_ps[:, 0:KD * P].rearrange("p (k n) -> p k n", k=KD),
                               ACT.Copy if phase == 0 else ACT.Relu).then_inc(hT_ready, 1)

                def p0(c):
                    if c % 2 == 0 and not first_block:
                        act.wait_ge(rows_saved[c // 2], 16 * n)
                    act.wait_ge(y_ready, CHUNKS * n + c + 1)
                    act.activation(rows_out[c // 2][:, 2 * (c % 2):2 * (c % 2) + 2, 0, :],
                                   y_ps[c][:, :].rearrange("p (r e) -> p r e", r=2), ACT.Copy).then_inc(part0, 1)

                def p1(c):
                    act.wait_ge(resid, CHUNKS + CHUNKS * n + c + 1)
                    act.activation(rows_out[c // 2][:, 2 * (c % 2):2 * (c % 2) + 2, 1, :], residual[c][:, :, :],
                                   ACT.Copy).then_inc(part1, 1)

                def save(half):
                    act.wait_ge(part2, CHUNKS * n + 2 * half + 2)
                    t = tables[phase % 2]
                    to = t[b] if isinstance(b, int) else t[bass.ds(b, 1)].rearrange("a p e -> (a p) e")
                    act.dma_start(to[:, half * HALF:(half + 1) * HALF],
                                  rows_out[half][:, :, :, :].rearrange("p r c e -> p (r c e)")) \
                        .then_inc(rows_saved[half], 16)

                p0(0)
                p0(1)
                p1(0)
                p0(2)
                p1(1)
                p0(3)
                save(0)
                p1(2)
                p1(3)
                save(1)

            act.wait_ge(small_T, 1)
            act.activation(b1_sb[:, :], comb_ps[:, 0:EX * KD], ACT.Copy).then_inc(small_out, 1)
            act.wait_ge(small_T, 2)
            act.activation(rw_sb[:, :, :], root_ps[:, 0:KD * EX].rearrange("p (k e) -> p k e", k=KD), ACT.Copy) \
                .then_inc(small_out, 1)

            def save_hots(i):
                for j in range(RING):
                    act.wait_ge(hot_made, RING * i + j + 1)
                    q = RING * i + j
                    to = onehots[q] if isinstance(q, int) else onehots[bass.ds(q, 1)].rearrange("a p e -> (a p) e")
                    act.dma_start(to, hot_ring[:, j * BATCH * P:(j + 1) * BATCH * P]).then_inc(hot_saved[j], 16)

            def root_of_variance(nth):
                act.wait_ge(var_ready, nth + 1)
                act.activation(std[:, :], var_eps[:, :], ACT.Sqrt).then_inc(std_ready, 1)

            root_of_variance(0)
            root_of_variance(1)
            post_table(0, 0, True)
            with act.Fori(2, BLOCKS) as b:
                root_of_variance(b)
                save_hots(b - 2)
                post_table(0, b - 1)
            save_hots(BLOCKS - 2)
            post_table(0, BLOCKS - 1)
            with act.Fori(BLOCKS - 1, Q) as i:
                save_hots(i)

            for phase in (1, 2):
                with act.Fori(0, BLOCKS) as b:
                    post_table(phase, b)

            def load_x(b):
                if isinstance(b, int) and b == BLOCKS - 1:
                    act.dma_start(x_sb[0:LAST, :], x[(BLOCKS - 1) * P:N, :]).then_inc(x_in, 16)
                elif isinstance(b, int):
                    act.dma_start(x_sb[:, :], x[b * P:(b + 1) * P, :]).then_inc(x_in, 16)
                else:
                    act.dma_start(x_sb[:, :], x[bass.ds(b * P, P), :]).then_inc(x_in, 16)

            def sigmoid(b):
                act.wait_ge(z_ready, b + 1)
                act.activation(sig_sb[:, :], z_sb[:, :], ACT.Sigmoid).then_inc(sig_ready, 1)

            def experts(b, last_block=False):
                n = n_of(3, b)
                act.wait_ge(transposed, n + 1)
                act.activation(hT[:, :, :], tr_ps[:, 0:KD * P].rearrange("p (k n) -> p k n", k=KD), ACT.Copy) \
                    .then_inc(hT_ready, 1)
                act.wait_ge(lmax_ok, b + 1)
                act.activation(pexp[:, :], root_ps[:, 0:EX], ACT.Exp, bias=nlmax[:, 0:1],
                               accum_out=psum_e[:, 0:1]).then_inc(pexp_ok, 1)
                for e in range(EX):
                    act.wait_ge(hid_ready, EX * b + e + 1)
                    for f in range(KD):
                        last = act.activation(hidden_sb[e % 2][:, f, :], y_ps[e % 2][:, f * P:(f + 1) * P],
                                              ACT.Gelu, bias=b1_sb[:, e * KD + f:e * KD + f + 1])
                    last.then_inc(gelu_done, 1)
                    if e == 1:
                        act.wait_ge(combT_ps, b + 1)
                        act.activation(combT[:, :], comb_ps[0:EX, 0:P], ACT.Copy).then_inc(combT_ok, 1)
                act.wait_ge(out_ready, b + 1)
                if last_block:
                    act.dma_start(out[(BLOCKS - 1) * P:N, :], out_sb[0:LAST, :]).then_inc(out_saved, 16)
                else:
                    act.dma_start(out[bass.ds(b * P, P), :], out_sb[:, :]).then_inc(out_saved, 16)

            load_x(0)
            sigmoid(0)
            act.wait_ge(x1_ready, 1)
            load_x(1)
            root_of_variance(BLOCKS)
            with act.Fori(1, BLOCKS - 2) as b:
                experts(b - 1)
                sigmoid(b)
                act.wait_ge(x1_ready, b + 1)
                load_x(b + 1)
                root_of_variance(BLOCKS + b)
                act.wait_ge(out_saved, 16 * b)
                act.sem_inc(out_free, 1)
            experts(BLOCKS - 3)
            sigmoid(BLOCKS - 2)
            act.wait_ge(x1_ready, BLOCKS - 1)
            load_x(BLOCKS - 1)
            root_of_variance(2 * BLOCKS - 2)
            act.wait_ge(out_saved, 16 * (BLOCKS - 2))
            act.sem_inc(out_free, 1)
            experts(BLOCKS - 2)
            sigmoid(BLOCKS - 1)
            root_of_variance(2 * BLOCKS - 1)
            act.wait_ge(out_saved, 16 * (BLOCKS - 1))
            act.sem_inc(out_free, 1)
            experts(BLOCKS - 1, True)
            act.wait_ge(out_saved, 16 * BLOCKS)

        @block.vector
        def _(dve):
            own = Chain(dve, dve_own)
            dve.memset(dst_i[:, :, :], PAD_NODE).then_inc(padded, 1)
            dve.memset(src_i[:, :, :], 0).then_inc(padded, 1)
            dve.memset(typ_i[:, :, :], 0).then_inc(padded, 1)
            dve.sem_inc(resid, CHUNKS)
            dve.sem_inc(root_taken, 1)
            dve.sem_inc(tile_free, SLOTS)
            dve.sem_inc(hot_free, SLOTS)
            dve.sem_inc(gelu_done, 2)
            dve.sem_inc(exp_taken, 2)
            dve.sem_inc(out_free, 1)

            full = E // (P * P)
            n_loads = 1 + ((E - full * P * P) // P > 0) + (E % P > 0)
            dve.wait_ge(edges_in, 16 * 3 * n_loads)
            dve.tensor_copy(dst_f[:, :, :], dst_i[:, :, :]).then_inc(edges_f, 1)
            dve.scalar_tensor_tensor(out=idx_f[:, :, :], in0=src_i[:, :, :], scalar=float(R), in1=typ_i[:, :, :],
                                     op0=ALU.mult, op1=ALU.add).then_inc(edges_f, 1)
            dve.wait_ge(consts, 7)
            own.link(dve.tensor_copy(iota_b[:, :], iota_i[:, :]))
            own.link(dve.tensor_copy(block_f[:, :], block_i[:, :]))
            own.link(dve.tensor_scalar(thresh[:, :], block_f[:, :], float(P), None, ALU.mult))
            own.link(dve.tensor_copy(step_f[:, :], step_i[:, :]))
            dve.wait_ge(edges_f, 1)
            own.link(dve.tensor_copy(last_f[:, :], dst_f[:, :, P - 1]))
            B1 = BLOCKS - 1
            own.link(dve.tensor_tensor(
                below[:, :, :], last_f[:, :].rearrange("p (b c) -> p b c", b=1).broadcast_to([P, B1, CH]),
                thresh[:, :].rearrange("p (b c) -> p b c", c=1).broadcast_to([P, B1, CH]), ALU.is_lt))
            dve.tensor_reduce(below_n[:, :], below[:, :, :], AX.X, ALU.add).then_inc(counted, 1)
            dve.wait_ge(totals, 1)
            own.link(dve.tensor_tensor(start_f[:, :], y_ps[0][:, 0:B1], block_f[:, :], ALU.add))
            own.link(dve.tensor_copy(bounds[0:1, 1:BLOCKS], y_ps[0][0:1, 0:B1]))
            own.link(dve.memset(bounds[0:1, 0:1], 0))
            dve.memset(bounds[0:1, BLOCKS:BLOCKS + 1], TILES - 1).then_inc(bounds_ok, 1)
            own.link(dve.tensor_tensor(
                reached[:, :, :], start_f[:, :].rearrange("p (c b) -> p c b", c=1).broadcast_to([P, CH, B1]),
                step_f[:, :].rearrange("p (c b) -> p c b", b=1).broadcast_to([P, CH, B1]), ALU.is_le))
            own.link(dve.tensor_reduce(block_of[:, :], reached[:, :, :], AX.X, ALU.add))
            own.link(dve.tensor_tensor(tile_f[:, :], step_f[:, :], block_of[:, :], ALU.subtract))
            dve.tensor_scalar(tile_of[:, :], tile_f[:, :], float(TILES - 1), None, ALU.min).then_inc(tiles_ok, 1)
            own.link(dve.tensor_scalar(beyond[:, :], step_f[:, :], float(STEPS), -2.0 * PAD_NODE, ALU.is_ge, ALU.mult))
            own.link(dve.scalar_tensor_tensor(out=shift[:, :], in0=block_of[:, :], scalar=-float(P),
                                              in1=beyond[:, :], op0=ALU.mult, op1=ALU.add))
            dve.wait_ge(dst_got, 16 * CH)
            for c in range(CH):
                dve.tensor_scalar(dst_sel[:, c, :], dst_sel[:, c, :], shift[:, c:c + 1], None, ALU.add) \
                    .then_inc(shifted, 1)
            for c in range(CH):
                dve.wait_ge(prep_T, c + 1)
                dve.tensor_copy(idx_all[:, c * P:(c + 1) * P], y_ps[c % 2][:, 0:P]).then_inc(prep_out, 1)
            for c in range(CH):
                dve.wait_ge(prep_T, CH + c + 1)
                dve.tensor_copy(loc_all[:, c * P:(c + 1) * P], y_ps[(CH + c) % 2][:, 0:P]).then_inc(prep_out, 1)
            links = own.k

            LN_LINKS = 3

            def layer_norm(source, nth):
                own.link(dve.bn_stats(stats[:, :], source[:, :]))
                dve.sem_inc(apart, 1)
                own.link(dve.bn_aggr(meanvar[:, :], stats[:, :]))
                dve.tensor_scalar(var_eps[:, :], meanvar[:, 1:2], EPS, None, ALU.add).then_inc(var_ready, 1)
                dve.wait_ge(std_ready, nth + 1)
                own.link(dve.reciprocal(rstd[:, :], std[:, :]))
                dve.tensor_scalar(h_sb[:, :], source[:, :], meanvar[:, 0:1], rstd[:, 0:1],
                                  ALU.subtract, ALU.mult).then_inc(h_ready, 1)

            def normalise(b, first_block=False):
                own.turn(links + LN_LINKS * b)
                dve.wait_ge(x_in, 16 * b + 16)
                if not first_block:
                    dve.wait_ge(transposed, b)
                layer_norm(x_sb, b)

            def post_table(phase, b):
                n = n_of(phase, b)

                def r1(c):
                    dve.wait_ge(part0, CHUNKS * n + c + 1)
                    dve.tensor_tensor(residual[c][:, :, :], y_ps[c][:, :].rearrange("p (r e) -> p r e", r=2),
                                      rows_out[c // 2][:, 2 * (c % 2):2 * (c % 2) + 2, 0, :],
                                      ALU.subtract).then_inc(resid, 1)

                def p2(c):
                    dve.wait_ge(part1, CHUNKS * n + c + 1)
                    dve.wait_ge(resid, CHUNKS + CHUNKS * n + c + 1)
                    dve.tensor_tensor(rows_out[c // 2][:, 2 * (c % 2):2 * (c % 2) + 2, 2, :],
                                      residual[c][:, :, :],
                                      rows_out[c // 2][:, 2 * (c % 2):2 * (c % 2) + 2, 1, :],
                                      ALU.subtract).then_inc(part2, 1)

                dve.wait_ge(root_taken, n + 1)
                r1(0)
                r1(1)
                p2(0)
                r1(2)
                p2(1)
                r1(3)
                p2(2)
                p2(3)
                dve.wait_ge(root_ready, n + 1)
                to = root_sb[:, bass.ds(b * D, D)] if not isinstance(b, int) else root_sb[:, b * D:(b + 1) * D]
                dve.tensor_tensor(to, root_ps[:, 0:D], bias_sb[:, phase, :], ALU.add).then_inc(root_taken, 1)

            def take_sum(phase, b, to):
                dve.wait_ge(agg_done, (phase - 1) * BLOCKS + b + 1)
                dve.wait_ge(root_taken, 1 + (phase - 1) * BLOCKS + b + 1)
                own_term = root_sb[:, bass.ds(b * D, D)] if not isinstance(b, int) else root_sb[:, b * D:(b + 1) * D]
                return dve.tensor_tensor(to[:, :], agg_ps[:, 0:D], own_term, ALU.add)

            Q = NQ // RING
            node_bc = iota_b[:, :].rearrange("p (u e) -> p u e", u=1).broadcast_to([P, BATCH, P])

            def make_hots(i, first_group=False):
                for j in range(RING):
                    if not first_group:
                        dve.wait_ge(hot_saved[j], 16 * i)
                    at = (RING * i + j) * BATCH
                    loc = loc_all[:, at:at + BATCH] if first_group else loc_all[:, bass.ds(at, BATCH)]
                    dve.tensor_tensor(hot4[:, j], node_bc,
                                      loc.rearrange("p (u e) -> p u e", e=1).broadcast_to([P, BATCH, P]),
                                      ALU.is_equal).then_inc(hot_made, 1)

            dve.wait_ge(weights_in, 16 * (4 + 2 * KD))
            dve.wait_ge(prep_out, 2 * CH)
            normalise(0, True)
            normalise(1)
            post_table(0, 0)
            make_hots(0, True)
            with dve.Fori(2, BLOCKS) as b:
                normalise(b)
                post_table(0, b - 1)
                make_hots(b - 1)
            post_table(0, BLOCKS - 1)
            with dve.Fori(BLOCKS - 1, Q) as i:
                make_hots(i)
            links += LN_LINKS * BLOCKS

            for phase in (1, 2):
                def h_block(b):
                    if not (phase == 1 and isinstance(b, int) and b == 0):
                        dve.wait_ge(transposed, n_of(phase, b))
                    take_sum(phase, b, h_sb).then_inc(h_ready, 1)

                h_block(0)
                with dve.Fori(1, BLOCKS) as b:
                    h_block(b)
                    post_table(phase, b - 1)
                post_table(phase, BLOCKS - 1)

            TOK_LINKS = LN_LINKS
            RT_LINKS = 15
            own.turn(links)
            own.link(dve.tensor_copy(desc8[:, :], iota_i[:, 0:EX]))
            own.link(dve.tensor_scalar(desc8[:, :], desc8[:, :], -1.0, float(EX), ALU.mult, ALU.add))
            links += 2

            def tokens(b):
                own.turn(links + (TOK_LINKS + RT_LINKS) * b)
                dve.wait_ge(sig_ready, b + 1)
                dve.wait_ge(x_in, 16 * (BLOCKS + b + 1))
                dve.tensor_tensor(x1_sb[:, :], x_sb[:, :], sig_sb[:, :], ALU.add).then_inc(x1_ready, 1)
                dve.wait_ge(x1_ready, b + 1)
                dve.wait_ge(transposed, n_of(3, b))
                layer_norm(x1_sb, BLOCKS + b)
                dve.wait_ge(h_ready, n_of(3, b) + 1)
                dve.tensor_tensor(acc_sb[:, :], x1_sb[:, :], h_sb[:, :], ALU.add).then_inc(acc_ready, 1)

            def route(b):
                own.turn(links + (TOK_LINKS + RT_LINKS) * b + TOK_LINKS)
                dve.wait_ge(logits, b + 1)
                own.link(dve.tensor_reduce(lmax[:, :], root_ps[:, 0:EX], AX.X, ALU.max))
                dve.tensor_scalar(nlmax[:, :], lmax[:, :], -1.0, None, ALU.mult).then_inc(lmax_ok, 1)
                dve.wait_ge(pexp_ok, b + 1)
                own.link(dve.reciprocal(rpsum[:, :], psum_e[:, :]))
                own.link(dve.tensor_scalar(probs[:, :], pexp[:, :], rpsum[:, 0:1], None, ALU.mult))
                own.link(dve.tensor_reduce(top[:, 0:1], probs[:, :], AX.X, ALU.max))
                own.link(dve.scalar_tensor_tensor(out=key[:, :], in0=probs[:, :], scalar=top[:, 0:1],
                                                  in1=desc8[:, :], op0=ALU.is_equal, op1=ALU.mult))
                own.link(dve.tensor_reduce(kmax[:, :], key[:, :], AX.X, ALU.max))
                own.link(dve.tensor_scalar(first[:, :], key[:, :], kmax[:, 0:1], None, ALU.is_equal))
                own.link(dve.scalar_tensor_tensor(out=rest[:, :], in0=first[:, :], scalar=-2.0,
                                                  in1=probs[:, :], op0=ALU.mult, op1=ALU.add))
                own.link(dve.tensor_reduce(top[:, 1:2], rest[:, :], AX.X, ALU.max))
                own.link(dve.scalar_tensor_tensor(out=key[:, :], in0=rest[:, :], scalar=top[:, 1:2],
                                                  in1=desc8[:, :], op0=ALU.is_equal, op1=ALU.mult))
                own.link(dve.tensor_reduce(kmax[:, :], key[:, :], AX.X, ALU.max))
                own.link(dve.scalar_tensor_tensor(out=chosen[:, :], in0=key[:, :], scalar=kmax[:, 0:1],
                                                  in1=first[:, :], op0=ALU.is_equal, op1=ALU.add))
                own.link(dve.tensor_tensor(second[:, :], chosen[:, :], probs[:, :], ALU.mult))
                own.link(dve.tensor_scalar(tsum[:, :], top[:, 0:1], top[:, 1:2], 1e-12, ALU.add, ALU.max))
                own.link(dve.reciprocal(rtsum[:, :], tsum[:, :]))
                assert own.k == RT_LINKS
                dve.tensor_scalar(comb[:, :], second[:, :], rtsum[:, 0:1], None, ALU.mult).then_inc(comb_ok, 1)

            def experts(b):
                dve.wait_ge(comb_ok, b + 1)
                for e in range(EX):
                    dve.wait_ge(acc_ready, (1 + EX) * b + 1 + e)
                    dve.wait_ge(exp_ready, EX * b + e + 1)
                    dve.scalar_tensor_tensor(out=acc_sb[:, :], in0=y_ps[2 + e % 2][:, 0:D], scalar=comb[:, e:e + 1],
                                             in1=acc_sb[:, :], op0=ALU.mult, op1=ALU.add).then_inc(acc_ready, 1)
                dve.wait_ge(acc_ready, (1 + EX) * (b + 1))
                dve.wait_ge(b2_ready, b + 1)
                dve.wait_ge(out_free, b + 1)
                dve.tensor_tensor(out_sb[:, :], acc_sb[:, :], root_ps[:, 0:D], ALU.add).then_inc(out_ready, 1)

            take_sum(3, 0, z_sb).then_inc(z_ready, 1)
            tokens(0)
            with dve.Fori(1, BLOCKS) as b:
                take_sum(3, b, z_sb).then_inc(z_ready, 1)
                route(b - 1)
                experts(b - 1)
                tokens(b)
            route(BLOCKS - 1)
            experts(BLOCKS - 1)

        @block.tensor
        def _(pe):
            def transposes(n):
                pe.wait_ge(h_ready, n + 1)
                for k in range(KD):
                    last = pe.transpose(tr_ps[:, k * P:(k + 1) * P], h_sb[:, k * P:(k + 1) * P], ident[:, :])
                last.then_inc(transposed, 1)
                pe.wait_ge(hT_ready, n + 1)

            pe.wait_ge(consts, 7)
            pe.wait_ge(weights_in, 16 * (4 + 2 * KD))
            pe.transpose(comb_ps[:, 0:EX * KD], b1_rows[:, :], ident[0:EX * KD, 0:EX * KD]).then_inc(small_T, 1)
            for k in range(KD):
                last = pe.transpose(root_ps[:, k * EX:(k + 1) * EX], rw_rows[:, k * P:(k + 1) * P],
                                    ident[0:EX, 0:EX])
            last.then_inc(small_T, 1)
            pe.wait_ge(counted, 1)
            pe.matmul(y_ps[0][:, 0:BLOCKS - 1], ones[:, :], below_n[:, :], start=True, stop=True).then_inc(totals, 1)
            pe.wait_ge(bounds_ok, 1)
            pe.wait_ge(edges_f, 2)
            for c in range(2 * CH):
                if c >= 2:
                    pe.wait_ge(prep_out, c - 1)
                if c >= CH:
                    pe.wait_ge(shifted, c - CH + 1)
                what = idx_f[:, c, :] if c < CH else dst_sel[:, c - CH, :]
                pe.transpose(y_ps[c % 2][:, 0:P], what, ident[:, :]).then_inc(prep_T, 1)
            pe.wait_ge(prep_out, 2 * CH)
            pe.wait_ge(small_out, 2)

            def post_table(phase, b):
                n = n_of(phase, b)
                transposes(n)
                for c in range(CHUNKS):
                    pe.wait_ge(resid, CHUNKS * n + c + 1)
                    for k in range(KD):
                        last = pe.matmul(y_ps[c][:, :], hT[:, k, :], gnn_w_sb[:, k, 2 * c:2 * c + 2, :]
                                         .rearrange("p r e -> p (r e)"), start=(k == 0), stop=(k == KD - 1))
                    last.then_inc(y_ready, 1)
                pe.wait_ge(root_taken, n + 1)
                for k in range(KD):
                    last = pe.matmul(root_ps[:, 0:D], hT[:, k, :], gnn_w_sb[:, k, R, :],
                                     start=(k == 0), stop=(k == KD - 1))
                last.then_inc(root_ready, 1)

            def steps(phase, b):
                layer = phase - 1
                if isinstance(b, int):
                    lo, hi_at = 0, bounds[0:1, b + 1:b + 2]
                else:
                    lo = pe.value_load(bounds[0:1, bass.ds(b, 1)], min_val=0, max_val=TILES - 1)
                    hi_at = bounds[0:1, bass.ds(b + 1, 1)]
                hi = pe.value_load(hi_at, min_val=0, max_val=TILES - 1)
                if not isinstance(b, int):
                    if phase < 3:
                        pe.wait_ge(h_ready, n_of(phase, b))
                    else:
                        pe.wait_ge(z_ready, b)
                pe.matmul(agg_ps[:, 0:D], zeros[:, 0:P], zeros[:, :], start=True, stop=False)

                def step(tile, passes_tile):
                    s = tile + b
                    pe.wait_ge(tile_ready, layer * TILES_P + tile + 1)
                    pe.wait_ge(hot_ready, layer * STEPS_P + s + 1)
                    if isinstance(s, int):
                        g0, o0 = (tile % SLOTS) * ROW, (s % SLOTS) * P
                        hot = hot_ring[:, o0:o0 + P]
                        part = lambda k: gathered[:, g0 + k * D:g0 + (k + 1) * D]
                    else:
                        g0 = pe.snap((tile % SLOTS) * ROW)
                        o0 = pe.snap((s % SLOTS) * P)
                        hot = hot_ring[:, bass.ds(o0, P)]
                        part = lambda k: gathered[:, bass.ds(g0 + k * D, D)]
                    for k in range(PARTS):
                        last = pe.matmul(agg_ps[:, 0:D], hot, part(k), start=False, stop=False)
                        if k == 0 and passes_tile:
                            last.then_inc(tile_free, 1)
                    last.then_inc(hot_free, 1)

                step(lo, False)
                with pe.If(hi > lo):
                    with pe.Fori(lo + 1, hi + 1) as tile:
                        step(tile, True)
                pe.matmul(agg_ps[:, 0:D], zeros[:, 0:P], zeros[:, :], start=False, stop=True).then_inc(agg_done, 1)

            def experts(b):
                transposes(n_of(3, b))
                for k in range(KD):
                    last = pe.matmul(root_ps[:, 0:EX], hT[:, k, :], rw_sb[:, k, :], start=(k == 0), stop=(k == KD - 1))
                last.then_inc(logits, 1)

                def hidden(e):
                    pe.wait_ge(gelu_done, EX * b + e + 1)
                    for f in range(KD):
                        for k in range(KD):
                            last = pe.matmul(y_ps[e % 2][:, f * P:(f + 1) * P],
                                             w1_sb[:, e, k, f * P:(f + 1) * P], hT[:, k, :],
                                             start=(k == 0), stop=(k == KD - 1))
                    last.then_inc(hid_ready, 1)

                def second_product(e):
                    pe.wait_ge(gelu_done, 2 + EX * b + e + 1)
                    if e < 2:
                        pe.wait_ge(comb_ok, b + 1)
                    pe.wait_ge(acc_ready, (1 + EX) * b + 1 + max(e - 1, 0))
                    for f in range(KD):
                        last = pe.matmul(y_ps[2 + e % 2][:, 0:D], hidden_sb[e % 2][:, f, :], w2_sb[:, e, f, :],
                                         start=(f == 0), stop=(f == KD - 1))
                    last.then_inc(exp_ready, 1)

                hidden(0)
                hidden(1)
                pe.wait_ge(comb_ok, b + 1)
                pe.transpose(comb_ps[0:EX, 0:P], comb[:, :], ident[:, :]).then_inc(combT_ps, 1)
                for e in range(EX):
                    second_product(e)
                    if e + 2 < EX:
                        hidden(e + 2)
                pe.wait_ge(combT_ok, b + 1)
                pe.matmul(root_ps[:, 0:D], combT[:, :], b2_sb[:, :], start=True, stop=True).then_inc(b2_ready, 1)

            for phase in range(4):
                if phase == 0:
                    pe.wait_ge(layer_w_in, 16 * 2 * KD)
                    with pe.Fori(0, BLOCKS) as b:
                        post_table(0, b)
                    continue
                post = experts if phase == 3 else (lambda b, phase=phase: post_table(phase, b))
                steps(phase, 0)
                if phase < 3:
                    pe.wait_ge(layer_w_in, 16 * 2 * KD * (phase + 1))
                with pe.Fori(1, BLOCKS) as b:
                    steps(phase, b)
                    post(b - 1)
                post(BLOCKS - 1)
                pe.matmul(agg_ps[:, 0:D], zeros[:, 0:P], zeros[:, :], start=True, stop=True) \
                    .then_inc(tile_free, TILES_P - (STEPS - BLOCKS))
                pe.matmul(agg_ps[:, 0:D], zeros[:, 0:P], zeros[:, :], start=True, stop=True) \
                    .then_inc(hot_free, STEPS_P - STEPS)


_INS = ["x", "src", "dst", "edge_type_8", "L0_gnn_weights", "L0_gnn_roots", "L0_gnn_biases", "L0_ffn_router_w",
        "L0_ffn_w1", "L0_ffn_b1", "L0_ffn_w2", "L0_ffn_b2"]


def kernel(**inputs):
    import numpy as _np
    import concourse.bacc as _bacc
    from concourse.bass_utils import run_bass_kernel_spmd as _run

    nc = _bacc.Bacc("TRN2", target_bir_lowering=False, num_devices=1)
    arrays, args = {}, []
    for name in _INS:
        a = _np.ascontiguousarray(inputs[name])
        arrays[f"in_{name}_dram"] = a
        args.append(nc.dram_tensor(f"in_{name}_dram", a.shape, mybir.dt.from_np(a.dtype), kind="ExternalInput").ap())
    out = nc.dram_tensor("out_dram", inputs["x"].shape, F32, kind="ExternalOutput").ap()
    gnn_moe(nc, *args, out)
    r = _run(nc, [arrays], core_ids=[0])
    return r.results[0]["out_dram"]
```

```python
from contextlib import ExitStack

import concourse.bass as bass
from concourse import mybir

ALU = mybir.AluOpType
ACT = mybir.ActivationFunctionType
AX = mybir.AxisListType
F32 = mybir.dt.float32
BF16 = mybir.dt.bfloat16
I32 = mybir.dt.int32
U32 = mybir.dt.uint32

P = 128
BATCH = 9
GROUP = 3
RING = 3
SLOTS = BATCH * RING
PARTS = 3
EPS = 1e-5


def round_up(n, m):
    return -(-n // m) * m


class Chain:

    def __init__(self, eng, sem):
        self.eng, self.sem, self.base, self.k = eng, sem, 0, 0

    def turn(self, base):
        self.base, self.k = base, 0

    def link(self, ins):
        self.k += 1
        ins.then_inc(self.sem, 1)
        self.eng.wait_ge(self.sem, self.base + self.k)


def gnn_moe(nc, x, src, dst, etype, gnn_w, gnn_root, gnn_bias, router_w, w1, b1, w2, b2, out):
    N, D = x.shape
    E = src.shape[0]
    LAYERS, R = gnn_w.shape[0], gnn_w.shape[1]
    EX = w1.shape[0]
    assert D == 256 and R == 8 and LAYERS == 3 and EX == 8
    KD = D // P
    BLOCKS = -(-N // P)
    LAST = N - (BLOCKS - 1) * P
    TILES = -(-E // P)
    GROUPS = -(-TILES // GROUP)
    FULL_GROUPS = E // (GROUP * P)
    STAGE = SLOTS
    TILES_P = round_up(TILES, 2 * STAGE)
    CH = -(-TILES_P // P)
    CG = -(-GROUPS // P)
    NQ = TILES_P // BATCH
    PAD_NODE = BLOCKS * P
    CHUNKS = R * D // 512
    ROW = PARTS * D
    HALF = R // 2 * ROW

    ctx = ExitStack()
    with ctx:
        def sb(name, shape, dt, where=ctx):
            return where.enter_context(nc.sbuf_tensor(name, shape, dt))

        def bank(name):
            return ctx.enter_context(nc.psum_tensor(name, [P, 512], F32))

        def sem(name):
            return ctx.enter_context(nc.semaphore(name))

        tables = [nc.dram_tensor(f"table{i}", [BLOCKS, P, R * ROW], BF16).ap() for i in range(2)]
        onehots = nc.dram_tensor("onehots", [NQ, P, BATCH * P], BF16).ap()
        dst_rows = nc.dram_tensor("dst_rows", [CH * P, P], F32).ap()

        ident = sb("ident", [P, P], F32)
        zeros = sb("zeros", [P, 2 * D], BF16)
        gnn_w_sb = sb("gnn_w_sb", [P, KD, R + 1, D], F32)
        bias_sb = sb("bias_sb", [P, LAYERS, D], F32)
        w1_sb = sb("w1_sb", [P, EX, KD, D], F32)
        w2_sb = sb("w2_sb", [P, EX, KD, D], F32)
        b1_rows = sb("b1_rows", [EX * KD, P], F32)
        b1_sb = sb("b1_sb", [P, EX * KD], F32)
        b2_sb = sb("b2_sb", [EX, D], F32)
        rw_rows = sb("rw_rows", [EX, D], F32)
        rw_sb = sb("rw_sb", [P, KD, EX], F32)
        root_sb = sb("root_sb", [P, BLOCKS * D], F32)
        idx_all = sb("idx_all", [P, CH * P], U32)
        stage_idx = [sb(f"stage_idx{i}", [P, STAGE], U32) for i in range(2)]
        hot_ring = sb("hot_ring", [P, SLOTS * P], BF16)
        shared_hot = sb("shared_hot", [P, GROUP * P], BF16)
        loc_shared = sb("loc_shared", [P, BLOCKS * GROUP], BF16)
        bounds = sb("bounds", [1, BLOCKS + 1], I32)
        x_sb = sb("x_sb", [P, D], F32)
        h_sb = sb("h_sb", [P, D], F32)
        hT = sb("hT", [P, KD, P], F32)
        residual = [sb(f"residual{i}", [P, 2, D], F32) for i in range(CHUNKS)]
        rows_out = [sb(f"rows_out{i}", [P, R // 2, PARTS, D], BF16) for i in range(2)]
        stats = sb("stats", [P, 6], F32)
        meanvar = sb("meanvar", [P, 2], F32)
        var_eps = sb("var_eps", [P, 1], F32)
        std = sb("std", [P, 1], F32)
        rstd = sb("rstd", [P, 1], F32)
        z_sb = sb("z_sb", [P, D], F32)
        sig_sb = sb("sig_sb", [P, D], F32)
        x1_sb = sb("x1_sb", [P, D], F32)
        acc_sb = sb("acc_sb", [P, D], F32)
        out_sb = sb("out_sb", [P, D], F32)
        hidden_sb = [sb(f"hidden_sb{i}", [P, KD, P], F32) for i in range(2)]
        combT = sb("combT", [EX, P], F32)
        desc8 = sb("desc8", [P, EX], F32)
        lmax = sb("lmax", [P, 1], F32)
        nlmax = sb("nlmax", [P, 1], F32)
        pexp = sb("pexp", [P, EX], F32)
        psum_e = sb("psum_e", [P, 1], F32)
        rpsum = sb("rpsum", [P, 1], F32)
        probs = sb("probs", [P, EX], F32)
        top = sb("top", [P, 2], F32)
        key = sb("key", [P, EX], F32)
        kmax = sb("kmax", [P, 1], F32)
        first = sb("first", [P, EX], F32)
        rest = sb("rest", [P, EX], F32)
        second = sb("second", [P, EX], F32)
        chosen = sb("chosen", [P, EX], F32)
        tsum = sb("tsum", [P, 1], F32)
        rtsum = sb("rtsum", [P, 1], F32)
        comb = sb("comb", [P, EX], F32)

        prep = ExitStack()
        dst_i = sb("dst_i", [P, CH, P], I32, prep)
        src_i = sb("src_i", [P, CH, P], I32, prep)
        typ_i = sb("typ_i", [P, CH, P], I32, prep)
        dst_f = sb("dst_f", [P, CH, P], F32, prep)
        idx_f = sb("idx_f", [P, CH, P], F32, prep)
        dst_loc = sb("dst_loc", [P, CH, P], F32, prep)
        dst_first = sb("dst_first", [BLOCKS - 1, GROUP, P], F32, prep)
        prep.close()
        assert (6 * CH + GROUP) * P * 4 <= SLOTS * ROW * 2
        gathered = sb("gathered", [P, SLOTS * ROW], BF16)
        ones = sb("ones", [P, P], F32)
        loc_all = sb("loc_all", [P, CH * P], BF16)
        iota_i = sb("iota_i", [P, P], I32)
        iota_b = sb("iota_b", [P, P], BF16)
        block_i = sb("block_i", [P, BLOCKS - 1], I32)
        block_f = sb("block_f", [P, BLOCKS - 1], F32)
        thresh = sb("thresh", [P, BLOCKS - 1], F32)
        last_i = sb("last_i", [P, CG, 2], I32)
        last_f = sb("last_f", [P, CG], F32)
        below = sb("below", [P, BLOCKS - 1, CG], F32)
        below_n = sb("below_n", [P, BLOCKS - 1], F32)
        start_f = sb("start_f", [P, BLOCKS - 1], F32)
        tile_i = sb("tile_i", [P, CH], I32)
        tile_f = sb("tile_f", [P, CH], F32)
        node0_i = sb("node0_i", [P, 1], I32)
        node0_f = sb("node0_f", [P, 1], F32)
        reached = sb("reached", [P, CH, BLOCKS - 1], F32)
        block_of = sb("block_of", [P, CH], F32)
        first_tiles = sb("first_tiles", [BLOCKS - 1, GROUP], U32)
        shift = sb("shift", [P, CH], F32)

        agg_ps = bank("agg_ps")
        tr_ps = bank("tr_ps")
        y_ps = [bank(f"y_ps{i}") for i in range(CHUNKS)]
        root_ps = bank("root_ps")
        comb_ps = bank("comb_ps")

        padded = sem("padded")
        edges_in = sem("edges_in")
        ends_in = sem("ends_in")
        weights_in = sem("weights_in")
        layer_w_in = sem("layer_w_in")
        consts = sem("consts")
        dve_own = sem("dve_own")
        edges_f = sem("edges_f")
        counted = sem("counted")
        totals = sem("totals")
        bounds_ok = sem("bounds_ok")
        tiles_ok = sem("tiles_ok")
        dst_saved = sem("dst_saved")
        dst_got = sem("dst_got")
        shifted = sem("shifted")
        prep_T = sem("prep_T")
        prep_out = sem("prep_out")
        hot_made = sem("hot_made")
        hot_saved = [sem(f"hot_saved{j}") for j in range(RING)]
        small_T = sem("small_T")
        small_out = sem("small_out")
        x_in = sem("x_in")
        apart = sem("apart")
        var_ready = sem("var_ready")
        std_ready = sem("std_ready")
        h_ready = sem("h_ready")
        transposed = sem("transposed")
        hT_ready = sem("hT_ready")
        y_ready = sem("y_ready")
        part0 = sem("part0")
        resid = sem("resid")
        part1 = sem("part1")
        part2 = sem("part2")
        rows_saved = [sem(f"rows_saved{i}") for i in range(2)]
        root_ready = sem("root_ready")
        root_taken = sem("root_taken")
        staged = sem("staged")
        tile_in = [sem(f"tile_in{j}") for j in range(RING)]
        tile_ready = sem("tile_ready")
        tile_free = sem("tile_free")
        hot_in = [sem(f"hot_in{j}") for j in range(RING)]
        hot_ready = sem("hot_ready")
        shared_ready = sem("shared_ready")
        half_sum = sem("half_sum")
        agg_done = sem("agg_done")
        z_ready = sem("z_ready")
        sig_ready = sem("sig_ready")
        x1_ready = sem("x1_ready")
        acc_ready = sem("acc_ready")
        logits = sem("logits")
        lmax_ok = sem("lmax_ok")
        pexp_ok = sem("pexp_ok")
        comb_ok = sem("comb_ok")
        combT_ps = sem("combT_ps")
        combT_ok = sem("combT_ok")
        hid_ready = sem("hid_ready")
        gelu_done = sem("gelu_done")
        exp_ready = sem("exp_ready")
        exp_taken = sem("exp_taken")
        b2_ready = sem("b2_ready")
        out_ready = sem("out_ready")
        out_free = sem("out_free")
        out_saved = sem("out_saved")

        def n_of(phase, b):
            return phase * BLOCKS + b

        def relu_rows(t):
            return t.rearrange("b p (r c) -> (b p r) c", r=R)

        hot4 = hot_ring[:, :].rearrange("p (q u e) -> p q u e", q=RING, u=BATCH)

        block = ctx.enter_context(nc.Block())

        @block.sync
        def _(sp):
            full = E // (P * P)
            rows = (E - full * P * P) // P
            tail = E - full * P * P - rows * P
            sp.wait_ge(padded, 4)
            for a, t in ((dst, dst_i), (src, src_i), (etype, typ_i)):
                sp.dma_start(t[:, 0:full, :], a[0:full * P * P].rearrange("(c p e) -> p c e", p=P, e=P)) \
                    .then_inc(edges_in, 16)
                if rows:
                    sp.dma_start(t[0:rows, full, :], a[full * P * P:full * P * P + rows * P]
                                 .rearrange("(p e) -> p e", e=P)).then_inc(edges_in, 16)
                if tail:
                    sp.dma_start(t[rows:rows + 1, full, 0:tail], a[E - tail:E].rearrange("(a e) -> a e", a=1)) \
                        .then_inc(edges_in, 16)

            def layer_weights(layer):
                for k in range(KD):
                    sp.dma_start(gnn_w_sb[:, k, 0:R, :], gnn_w[layer, :, k * P:(k + 1) * P, :]
                                 .rearrange("r p e -> p r e")).then_inc(layer_w_in, 16)
                    sp.dma_start(gnn_w_sb[:, k, R, :], gnn_root[layer, k * P:(k + 1) * P, :]) \
                        .then_inc(layer_w_in, 16)

            ends = dst[0:FULL_GROUPS * GROUP * P].rearrange("(g w) -> g w", w=GROUP * P)[:, GROUP * P - 2:]
            sp.dma_start(last_i[:, 0:FULL_GROUPS // P, :],
                         ends[0:FULL_GROUPS // P * P].rearrange("(c p) w -> p c w", p=P)).then_inc(ends_in, 16)
            sp.dma_start(last_i[0:FULL_GROUPS % P, FULL_GROUPS // P, :], ends[FULL_GROUPS // P * P:FULL_GROUPS]) \
                .then_inc(ends_in, 16)

            layer_weights(0)
            sp.dma_start(x_sb[:, :], x[0:P, :]).then_inc(x_in, 16)
            sp.dma_start(bias_sb[:, :, :], gnn_bias.rearrange("(a l) d -> a l d", a=1).broadcast_to([P, LAYERS, D])) \
                .then_inc(weights_in, 16)
            sp.dma_start(b1_rows[:, :], b1.rearrange("e (k p) -> (e k) p", p=P)).then_inc(weights_in, 16)
            sp.dma_start(rw_rows[:, :], router_w).then_inc(weights_in, 16)
            sp.dma_start(b2_sb[:, :], b2).then_inc(weights_in, 16)
            for k in range(KD):
                sp.dma_start(w1_sb[:, :, k, :], w1[:, k * P:(k + 1) * P, :].rearrange("e p f -> p e f")) \
                    .then_inc(weights_in, 16)
                sp.dma_start(w2_sb[:, :, k, :], w2[:, k * P:(k + 1) * P, :].rearrange("e p f -> p e f")) \
                    .then_inc(weights_in, 16)

            sp.wait_ge(edges_f, 1)
            sp.dma_start(dst_rows.rearrange("(c p) e -> p c e", p=P), dst_f[:, :, :]).then_inc(dst_saved, 16)

            with sp.Fori(1, BLOCKS - 1) as b:
                sp.wait_ge(h_ready, b)
                sp.dma_start(x_sb[:, :], x[bass.ds(b * P, P), :]).then_inc(x_in, 16)
            sp.wait_ge(h_ready, BLOCKS - 1)
            sp.dma_start(x_sb[0:LAST, :], x[(BLOCKS - 1) * P:N, :]).then_inc(x_in, 16)

            for j in range(RING):
                sp.wait_ge(hot_saved[j], 16 * (NQ // RING))
            for layer in range(LAYERS):
                if layer + 1 < LAYERS:
                    sp.wait_ge(root_ready, (layer + 1) * BLOCKS)
                    layer_weights(layer + 1)

                def issue(q, j):
                    sp.wait_ge(tile_free, layer * TILES_P + BATCH * q + BATCH)
                    src_ap = onehots[q] if isinstance(q, int) else onehots[bass.ds(q, 1)].rearrange("a p e -> (a p) e")
                    sp.dma_start(hot_ring[:, j * BATCH * P:(j + 1) * BATCH * P], src_ap).then_inc(hot_in[j], 16)

                def ready(i, j):
                    sp.wait_ge(hot_in[j], 16 * (layer * (NQ // RING) + i + 1))
                    sp.sem_inc(hot_ready, BATCH)

                issue(0, 0)
                with sp.Fori(0, NQ // RING - 1) as i:
                    for j in range(RING):
                        issue(RING * i + j + 1, (j + 1) % RING)
                        ready(i, j)
                for j in range(1, RING):
                    issue(NQ - RING + j, j)
                    ready(NQ // RING - 1, j - 1)
                ready(NQ // RING - 1, RING - 1)

        @block.gpsimd
        def _(pool):
            pool.memset(ident[:, :], 0.0).then_inc(consts, 1)
            pool.wait_ge(consts, 1)
            pool.affine_select(out=ident[:, :], in_=ident[:, :], compare_op=ALU.not_equal, fill=1.0,
                               base=0, pattern=[[-1, P]], channel_multiplier=1).then_inc(consts, 1)
            pool.iota(iota_i[:, :], pattern=[[1, P]], base=0, channel_multiplier=0).then_inc(consts, 1)
            pool.iota(block_i[:, :], pattern=[[1, BLOCKS - 1]], base=1, channel_multiplier=0).then_inc(consts, 1)
            pool.iota(tile_i[:, :], pattern=[[P, CH]], base=0, channel_multiplier=1).then_inc(consts, 1)
            pool.iota(node0_i[:, :], pattern=[[0, 1]], base=P, channel_multiplier=P).then_inc(consts, 1)
            pool.memset(ones[:, :], 1.0).then_inc(consts, 1)
            pool.memset(zeros[:, :], 0.0).then_inc(consts, 1)

            pool.wait_ge(tiles_ok, GROUP)
            pool.wait_ge(dst_saved, 16)
            for g in range(GROUP):
                pool.indirect_dma_start(out=dst_first[:, g, :], out_offset=None, in_=dst_rows,
                                        in_offset=bass.IndirectOffsetOnAxis(ap=first_tiles[:, g:g + 1], axis=0)) \
                    .then_inc(dst_got, 16)

            GQ = TILES_P // BATCH
            HALVES = TILES_P // STAGE

            def stage(half, s):
                at = half * STAGE
                cols = idx_all[:, bass.ds(at, STAGE)] if not isinstance(half, int) else idx_all[:, at:at + STAGE]
                pool.tensor_copy(stage_idx[s][:, :], cols).then_inc(staged, 1)

            for layer in range(LAYERS):
                rows_of = relu_rows(tables[layer % 2])

                def landed(turns, j):
                    pool.wait_ge(tile_in[j], 16 * BATCH * (layer * (GQ // RING) + turns))
                    pool.sem_inc(tile_ready, BATCH)

                def half_gathers(half, s, first_half, last_half):
                    pool.wait_ge(staged, layer * HALVES + half + 1)
                    for j in range(RING):
                        pool.wait_ge(tile_free, layer * TILES_P + STAGE * half + BATCH * (j + 1))
                        pool.wait_ge(rows_saved[0], 16 * BLOCKS * (layer + 1))
                        pool.wait_ge(rows_saved[1], 16 * BLOCKS * (layer + 1))
                        pool.sem_inc(apart, 1)
                        for u in range(BATCH):
                            n = j * BATCH + u
                            pool.indirect_dma_start(
                                out=gathered[:, n * ROW:(n + 1) * ROW], out_offset=None, in_=rows_of,
                                in_offset=bass.IndirectOffsetOnAxis(ap=stage_idx[s][:, n:n + 1], axis=0)) \
                                .then_inc(tile_in[j], 16)
                            if u == 2 and not (first_half and j == 0):
                                landed(half if j == 0 else half + 1, (j - 1) % RING)
                            if u == 4 and j == 1 and not last_half:
                                stage(half + 1, 1 - s)

                if layer == 0:
                    pool.wait_ge(prep_out, 2 * CH + 1)
                stage(0, 0)
                half_gathers(0, 0, True, False)
                half_gathers(1, 1, False, False)
                with pool.Fori(1, HALVES // 2 - 1) as i:
                    half_gathers(2 * i, 0, False, False)
                    half_gathers(2 * i + 1, 1, False, False)
                half_gathers(HALVES - 2, 0, False, False)
                half_gathers(HALVES - 1, 1, False, True)
                landed(HALVES, RING - 1)

        @block.scalar
        def _(act):
            Q = NQ // RING

            def post_table(phase, b, first_block=False):
                n = n_of(phase, b)
                act.wait_ge(transposed, n + 1)
                act.activation(hT[:, :, :], tr_ps[:, 0:KD * P].rearrange("p (k n) -> p k n", k=KD),
                               ACT.Copy if phase == 0 else ACT.Relu).then_inc(hT_ready, 1)

                def p0(c):
                    if c % 2 == 0 and not first_block:
                        act.wait_ge(rows_saved[c // 2], 16 * n)
                    act.wait_ge(y_ready, CHUNKS * n + c + 1)
                    act.activation(rows_out[c // 2][:, 2 * (c % 2):2 * (c % 2) + 2, 0, :],
                                   y_ps[c][:, :].rearrange("p (r e) -> p r e", r=2), ACT.Copy).then_inc(part0, 1)

                def p1(c):
                    act.wait_ge(resid, CHUNKS + CHUNKS * n + c + 1)
                    act.activation(rows_out[c // 2][:, 2 * (c % 2):2 * (c % 2) + 2, 1, :], residual[c][:, :, :],
                                   ACT.Copy).then_inc(part1, 1)

                def save(half):
                    act.wait_ge(part2, CHUNKS * n + 2 * half + 2)
                    t = tables[phase % 2]
                    to = t[b] if isinstance(b, int) else t[bass.ds(b, 1)].rearrange("a p e -> (a p) e")
                    act.dma_start(to[:, half * HALF:(half + 1) * HALF],
                                  rows_out[half][:, :, :, :].rearrange("p r c e -> p (r c e)")) \
                        .then_inc(rows_saved[half], 16)

                p0(0)
                p0(1)
                p1(0)
                p0(2)
                p1(1)
                p0(3)
                save(0)
                p1(2)
                p1(3)
                save(1)

            act.wait_ge(small_T, 1)
            act.activation(b1_sb[:, :], comb_ps[:, 0:EX * KD], ACT.Copy).then_inc(small_out, 1)
            act.wait_ge(small_T, 2)
            act.activation(rw_sb[:, :, :], root_ps[:, 0:KD * EX].rearrange("p (k e) -> p k e", k=KD), ACT.Copy) \
                .then_inc(small_out, 1)

            def save_hots(i):
                for j in range(RING):
                    act.wait_ge(hot_made, RING * i + j + 1)
                    q = RING * i + j
                    to = onehots[q] if isinstance(q, int) else onehots[bass.ds(q, 1)].rearrange("a p e -> (a p) e")
                    act.dma_start(to, hot_ring[:, j * BATCH * P:(j + 1) * BATCH * P]).then_inc(hot_saved[j], 16)

            def root_of_variance(nth):
                act.wait_ge(var_ready, nth + 1)
                act.activation(std[:, :], var_eps[:, :], ACT.Sqrt).then_inc(std_ready, 1)

            root_of_variance(0)
            root_of_variance(1)
            post_table(0, 0, True)
            with act.Fori(2, BLOCKS) as b:
                root_of_variance(b)
                save_hots(b - 2)
                post_table(0, b - 1)
            save_hots(BLOCKS - 2)
            post_table(0, BLOCKS - 1)
            with act.Fori(BLOCKS - 1, Q) as i:
                save_hots(i)

            for phase in (1, 2):
                with act.Fori(0, BLOCKS) as b:
                    post_table(phase, b)

            def load_x(b):
                if isinstance(b, int) and b == BLOCKS - 1:
                    act.dma_start(x_sb[0:LAST, :], x[(BLOCKS - 1) * P:N, :]).then_inc(x_in, 16)
                elif isinstance(b, int):
                    act.dma_start(x_sb[:, :], x[b * P:(b + 1) * P, :]).then_inc(x_in, 16)
                else:
                    act.dma_start(x_sb[:, :], x[bass.ds(b * P, P), :]).then_inc(x_in, 16)

            def sigmoid(b):
                act.wait_ge(z_ready, b + 1)
                act.activation(sig_sb[:, :], z_sb[:, :], ACT.Sigmoid).then_inc(sig_ready, 1)

            def experts(b, last_block=False):
                n = n_of(3, b)
                act.wait_ge(transposed, n + 1)
                act.activation(hT[:, :, :], tr_ps[:, 0:KD * P].rearrange("p (k n) -> p k n", k=KD), ACT.Copy) \
                    .then_inc(hT_ready, 1)
                act.wait_ge(lmax_ok, b + 1)
                act.activation(pexp[:, :], root_ps[:, 0:EX], ACT.Exp, bias=nlmax[:, 0:1],
                               accum_out=psum_e[:, 0:1]).then_inc(pexp_ok, 1)
                for e in range(EX):
                    act.wait_ge(hid_ready, EX * b + e + 1)
                    for f in range(KD):
                        last = act.activation(hidden_sb[e % 2][:, f, :], y_ps[e % 2][:, f * P:(f + 1) * P],
                                              ACT.Gelu, bias=b1_sb[:, e * KD + f:e * KD + f + 1])
                    last.then_inc(gelu_done, 1)
                    if e == 1:
                        act.wait_ge(combT_ps, b + 1)
                        act.activation(combT[:, :], comb_ps[0:EX, 0:P], ACT.Copy).then_inc(combT_ok, 1)
                act.wait_ge(out_ready, b + 1)
                if last_block:
                    act.dma_start(out[(BLOCKS - 1) * P:N, :], out_sb[0:LAST, :]).then_inc(out_saved, 16)
                else:
                    act.dma_start(out[bass.ds(b * P, P), :], out_sb[:, :]).then_inc(out_saved, 16)

            load_x(0)
            sigmoid(0)
            act.wait_ge(x1_ready, 1)
            load_x(1)
            root_of_variance(BLOCKS)
            with act.Fori(1, BLOCKS - 2) as b:
                experts(b - 1)
                sigmoid(b)
                act.wait_ge(x1_ready, b + 1)
                load_x(b + 1)
                root_of_variance(BLOCKS + b)
                act.wait_ge(out_saved, 16 * b)
                act.sem_inc(out_free, 1)
            experts(BLOCKS - 3)
            sigmoid(BLOCKS - 2)
            act.wait_ge(x1_ready, BLOCKS - 1)
            load_x(BLOCKS - 1)
            root_of_variance(2 * BLOCKS - 2)
            act.wait_ge(out_saved, 16 * (BLOCKS - 2))
            act.sem_inc(out_free, 1)
            experts(BLOCKS - 2)
            sigmoid(BLOCKS - 1)
            root_of_variance(2 * BLOCKS - 1)
            act.wait_ge(out_saved, 16 * (BLOCKS - 1))
            act.sem_inc(out_free, 1)
            experts(BLOCKS - 1, True)
            act.wait_ge(out_saved, 16 * BLOCKS)

        @block.vector
        def _(dve):
            own = Chain(dve, dve_own)
            dve.memset(dst_i[:, :, :], PAD_NODE).then_inc(padded, 1)
            dve.memset(src_i[:, :, :], 0).then_inc(padded, 1)
            dve.memset(typ_i[:, :, :], 0).then_inc(padded, 1)
            dve.memset(last_i[:, :, :], PAD_NODE).then_inc(padded, 1)
            own.link(dve.memset(loc_shared[:, :], -1.0))
            dve.sem_inc(resid, CHUNKS)
            dve.sem_inc(root_taken, 1)
            dve.sem_inc(tile_free, SLOTS)
            dve.sem_inc(gelu_done, 2)
            dve.sem_inc(exp_taken, 2)
            dve.sem_inc(out_free, 1)

            full = E // (P * P)
            n_loads = 1 + ((E - full * P * P) // P > 0) + (E % P > 0)
            dve.wait_ge(edges_in, 16 * 3 * n_loads)
            dve.tensor_copy(dst_f[:, :, :], dst_i[:, :, :]).then_inc(edges_f, 1)
            dve.scalar_tensor_tensor(out=idx_f[:, :, :], in0=src_i[:, :, :], scalar=float(R), in1=typ_i[:, :, :],
                                     op0=ALU.mult, op1=ALU.add).then_inc(edges_f, 1)
            dve.wait_ge(consts, 8)
            own.link(dve.tensor_copy(iota_b[:, :], iota_i[:, :]))
            own.link(dve.tensor_copy(block_f[:, :], block_i[:, :]))
            own.link(dve.tensor_scalar(thresh[:, :], block_f[:, :], float(P), None, ALU.mult))
            own.link(dve.tensor_copy(tile_f[:, :], tile_i[:, :]))
            own.link(dve.tensor_copy(node0_f[:, :], node0_i[:, :]))
            dve.wait_ge(ends_in, 16 * 2)
            own.link(dve.tensor_copy(last_f[:, :], last_i[:, :, 1]))
            B1 = BLOCKS - 1
            own.link(dve.tensor_tensor(
                below[:, :, :], last_f[:, :].rearrange("p (b c) -> p b c", b=1).broadcast_to([P, B1, CG]),
                thresh[:, :].rearrange("p (b c) -> p b c", c=1).broadcast_to([P, B1, CG]), ALU.is_lt))
            dve.tensor_reduce(below_n[:, :], below[:, :, :], AX.X, ALU.add).then_inc(counted, 1)
            dve.wait_ge(totals, 1)
            for g in range(GROUP):
                dve.tensor_scalar(first_tiles[:, g:g + 1], y_ps[1][0:B1, 0:1], float(GROUP), float(g),
                                  ALU.mult, ALU.add).then_inc(tiles_ok, 1)
            own.link(dve.tensor_scalar(start_f[:, :], y_ps[0][:, 0:B1], float(GROUP), float(GROUP),
                                       ALU.mult, ALU.add))
            own.link(dve.tensor_copy(bounds[0:1, 1:BLOCKS], y_ps[0][0:1, 0:B1]))
            own.link(dve.memset(bounds[0:1, 0:1], 0))
            dve.memset(bounds[0:1, BLOCKS:BLOCKS + 1], GROUPS - 1).then_inc(bounds_ok, 1)
            own.link(dve.tensor_tensor(
                reached[:, :, :], start_f[:, :].rearrange("p (c b) -> p c b", c=1).broadcast_to([P, CH, B1]),
                tile_f[:, :].rearrange("p (c b) -> p c b", b=1).broadcast_to([P, CH, B1]), ALU.is_le))
            own.link(dve.tensor_reduce(block_of[:, :], reached[:, :, :], AX.X, ALU.add))
            own.link(dve.tensor_scalar(shift[:, :], block_of[:, :], -float(P), None, ALU.mult))
            for c in range(CH):
                dve.tensor_scalar(dst_loc[:, c, :], dst_f[:, c, :], shift[:, c:c + 1], None, ALU.add) \
                    .then_inc(shifted, 1)
            dve.wait_ge(dst_got, 16 * GROUP)
            dve.tensor_scalar(dst_first[:, :, :], dst_first[:, :, :], node0_f[0:B1, 0:1], None, ALU.subtract) \
                .then_inc(shifted, 1)
            for c in range(CH):
                dve.wait_ge(prep_T, c + 1)
                dve.tensor_copy(idx_all[:, c * P:(c + 1) * P], y_ps[c % 2][:, 0:P]).then_inc(prep_out, 1)
            for c in range(CH):
                dve.wait_ge(prep_T, CH + c + 1)
                dve.tensor_copy(loc_all[:, c * P:(c + 1) * P], y_ps[(CH + c) % 2][:, 0:P]).then_inc(prep_out, 1)
            dve.wait_ge(prep_T, 2 * CH + 1)
            dve.tensor_copy(loc_shared[:, 0:B1 * GROUP].rearrange("p (b g) -> p b g", g=GROUP),
                            y_ps[0][:, 0:B1 * GROUP].rearrange("p (g b) -> p b g", g=GROUP)).then_inc(prep_out, 1)
            links = own.k

            LN_LINKS = 3

            def layer_norm(source, nth):
                own.link(dve.bn_stats(stats[:, :], source[:, :]))
                dve.sem_inc(apart, 1)
                own.link(dve.bn_aggr(meanvar[:, :], stats[:, :]))
                dve.tensor_scalar(var_eps[:, :], meanvar[:, 1:2], EPS, None, ALU.add).then_inc(var_ready, 1)
                dve.wait_ge(std_ready, nth + 1)
                own.link(dve.reciprocal(rstd[:, :], std[:, :]))
                dve.tensor_scalar(h_sb[:, :], source[:, :], meanvar[:, 0:1], rstd[:, 0:1],
                                  ALU.subtract, ALU.mult).then_inc(h_ready, 1)

            def normalise(b, first_block=False):
                own.turn(links + LN_LINKS * b)
                dve.wait_ge(x_in, 16 * b + 16)
                if not first_block:
                    dve.wait_ge(transposed, b)
                layer_norm(x_sb, b)

            def post_table(phase, b):
                n = n_of(phase, b)

                def r1(c):
                    dve.wait_ge(part0, CHUNKS * n + c + 1)
                    dve.tensor_tensor(residual[c][:, :, :], y_ps[c][:, :].rearrange("p (r e) -> p r e", r=2),
                                      rows_out[c // 2][:, 2 * (c % 2):2 * (c % 2) + 2, 0, :],
                                      ALU.subtract).then_inc(resid, 1)

                def p2(c):
                    dve.wait_ge(part1, CHUNKS * n + c + 1)
                    dve.wait_ge(resid, CHUNKS + CHUNKS * n + c + 1)
                    dve.tensor_tensor(rows_out[c // 2][:, 2 * (c % 2):2 * (c % 2) + 2, 2, :],
                                      residual[c][:, :, :],
                                      rows_out[c // 2][:, 2 * (c % 2):2 * (c % 2) + 2, 1, :],
                                      ALU.subtract).then_inc(part2, 1)

                dve.wait_ge(root_taken, n + 1)
                r1(0)
                r1(1)
                p2(0)
                r1(2)
                p2(1)
                r1(3)
                p2(2)
                p2(3)
                dve.wait_ge(root_ready, n + 1)
                to = root_sb[:, bass.ds(b * D, D)] if not isinstance(b, int) else root_sb[:, b * D:(b + 1) * D]
                dve.tensor_tensor(to, root_ps[:, 0:D], bias_sb[:, phase, :], ALU.add).then_inc(root_taken, 1)

            def take_sum(phase, b, to):
                dve.wait_ge(agg_done, (phase - 1) * BLOCKS + b + 1)
                dve.wait_ge(root_taken, 1 + (phase - 1) * BLOCKS + b + 1)
                own_term = root_sb[:, bass.ds(b * D, D)] if not isinstance(b, int) else root_sb[:, b * D:(b + 1) * D]
                dve.tensor_tensor(own_term, agg_ps[:, 0:D], own_term, ALU.add).then_inc(half_sum, 1)
                dve.wait_ge(half_sum, (phase - 1) * BLOCKS + b + 1)
                return dve.tensor_tensor(to[:, :], agg_ps[:, D:2 * D], own_term, ALU.add)

            group_bc = iota_b[:, :].rearrange("p (u e) -> p u e", u=1).broadcast_to([P, GROUP, P])

            def make_shared(b):
                loc = loc_shared[:, bass.ds((b - 1) * GROUP, GROUP)] if not isinstance(b, int) else \
                    loc_shared[:, (b - 1) * GROUP:b * GROUP]
                dve.tensor_tensor(shared_hot[:, :].rearrange("p (u e) -> p u e", u=GROUP), group_bc,
                                  loc.rearrange("p (u e) -> p u e", e=1).broadcast_to([P, GROUP, P]),
                                  ALU.is_equal).then_inc(shared_ready, 1)

            Q = NQ // RING
            node_bc = iota_b[:, :].rearrange("p (u e) -> p u e", u=1).broadcast_to([P, BATCH, P])

            def make_hots(i, first_group=False):
                for j in range(RING):
                    if not first_group:
                        dve.wait_ge(hot_saved[j], 16 * i)
                    at = (RING * i + j) * BATCH
                    loc = loc_all[:, at:at + BATCH] if first_group else loc_all[:, bass.ds(at, BATCH)]
                    dve.tensor_tensor(hot4[:, j], node_bc,
                                      loc.rearrange("p (u e) -> p u e", e=1).broadcast_to([P, BATCH, P]),
                                      ALU.is_equal).then_inc(hot_made, 1)

            dve.wait_ge(weights_in, 16 * (4 + 2 * KD))
            dve.wait_ge(prep_out, 2 * CH + 1)
            normalise(0, True)
            normalise(1)
            post_table(0, 0)
            make_hots(0, True)
            with dve.Fori(2, BLOCKS) as b:
                normalise(b)
                post_table(0, b - 1)
                make_hots(b - 1)
            post_table(0, BLOCKS - 1)
            with dve.Fori(BLOCKS - 1, Q) as i:
                make_hots(i)
            links += LN_LINKS * BLOCKS

            for phase in (1, 2):
                def h_block(b):
                    if not (phase == 1 and isinstance(b, int) and b == 0):
                        dve.wait_ge(transposed, n_of(phase, b))
                    take_sum(phase, b, h_sb).then_inc(h_ready, 1)
                    make_shared(b + 1)

                h_block(0)
                with dve.Fori(1, BLOCKS) as b:
                    h_block(b)
                    post_table(phase, b - 1)
                post_table(phase, BLOCKS - 1)

            TOK_LINKS = LN_LINKS
            RT_LINKS = 15
            own.turn(links)
            own.link(dve.tensor_copy(desc8[:, :], iota_i[:, 0:EX]))
            own.link(dve.tensor_scalar(desc8[:, :], desc8[:, :], -1.0, float(EX), ALU.mult, ALU.add))
            links += 2

            def tokens(b):
                own.turn(links + (TOK_LINKS + RT_LINKS) * b)
                dve.wait_ge(sig_ready, b + 1)
                dve.wait_ge(x_in, 16 * (BLOCKS + b + 1))
                dve.tensor_tensor(x1_sb[:, :], x_sb[:, :], sig_sb[:, :], ALU.add).then_inc(x1_ready, 1)
                dve.wait_ge(x1_ready, b + 1)
                dve.wait_ge(transposed, n_of(3, b))
                layer_norm(x1_sb, BLOCKS + b)
                dve.wait_ge(h_ready, n_of(3, b) + 1)
                dve.tensor_tensor(acc_sb[:, :], x1_sb[:, :], h_sb[:, :], ALU.add).then_inc(acc_ready, 1)

            def route(b):
                own.turn(links + (TOK_LINKS + RT_LINKS) * b + TOK_LINKS)
                dve.wait_ge(logits, b + 1)
                own.link(dve.tensor_reduce(lmax[:, :], root_ps[:, 0:EX], AX.X, ALU.max))
                dve.tensor_scalar(nlmax[:, :], lmax[:, :], -1.0, None, ALU.mult).then_inc(lmax_ok, 1)
                dve.wait_ge(pexp_ok, b + 1)
                own.link(dve.reciprocal(rpsum[:, :], psum_e[:, :]))
                own.link(dve.tensor_scalar(probs[:, :], pexp[:, :], rpsum[:, 0:1], None, ALU.mult))
                own.link(dve.tensor_reduce(top[:, 0:1], probs[:, :], AX.X, ALU.max))
                own.link(dve.scalar_tensor_tensor(out=key[:, :], in0=probs[:, :], scalar=top[:, 0:1],
                                                  in1=desc8[:, :], op0=ALU.is_equal, op1=ALU.mult))
                own.link(dve.tensor_reduce(kmax[:, :], key[:, :], AX.X, ALU.max))
                own.link(dve.tensor_scalar(first[:, :], key[:, :], kmax[:, 0:1], None, ALU.is_equal))
                own.link(dve.scalar_tensor_tensor(out=rest[:, :], in0=first[:, :], scalar=-2.0,
                                                  in1=probs[:, :], op0=ALU.mult, op1=ALU.add))
                own.link(dve.tensor_reduce(top[:, 1:2], rest[:, :], AX.X, ALU.max))
                own.link(dve.scalar_tensor_tensor(out=key[:, :], in0=rest[:, :], scalar=top[:, 1:2],
                                                  in1=desc8[:, :], op0=ALU.is_equal, op1=ALU.mult))
                own.link(dve.tensor_reduce(kmax[:, :], key[:, :], AX.X, ALU.max))
                own.link(dve.scalar_tensor_tensor(out=chosen[:, :], in0=key[:, :], scalar=kmax[:, 0:1],
                                                  in1=first[:, :], op0=ALU.is_equal, op1=ALU.add))
                own.link(dve.tensor_tensor(second[:, :], chosen[:, :], probs[:, :], ALU.mult))
                own.link(dve.tensor_scalar(tsum[:, :], top[:, 0:1], top[:, 1:2], 1e-12, ALU.add, ALU.max))
                own.link(dve.reciprocal(rtsum[:, :], tsum[:, :]))
                assert own.k == RT_LINKS
                dve.tensor_scalar(comb[:, :], second[:, :], rtsum[:, 0:1], None, ALU.mult).then_inc(comb_ok, 1)

            def experts(b):
                dve.wait_ge(comb_ok, b + 1)
                for e in range(EX):
                    dve.wait_ge(acc_ready, (1 + EX) * b + 1 + e)
                    dve.wait_ge(exp_ready, EX * b + e + 1)
                    dve.scalar_tensor_tensor(out=acc_sb[:, :], in0=y_ps[2 + e % 2][:, 0:D], scalar=comb[:, e:e + 1],
                                             in1=acc_sb[:, :], op0=ALU.mult, op1=ALU.add).then_inc(acc_ready, 1)
                dve.wait_ge(acc_ready, (1 + EX) * (b + 1))
                dve.wait_ge(b2_ready, b + 1)
                dve.wait_ge(out_free, b + 1)
                dve.tensor_tensor(out_sb[:, :], acc_sb[:, :], root_ps[:, 0:D], ALU.add).then_inc(out_ready, 1)

            take_sum(3, 0, z_sb).then_inc(z_ready, 1)
            make_shared(1)
            tokens(0)
            with dve.Fori(1, BLOCKS) as b:
                take_sum(3, b, z_sb).then_inc(z_ready, 1)
                make_shared(b + 1)
                route(b - 1)
                experts(b - 1)
                tokens(b)
            route(BLOCKS - 1)
            experts(BLOCKS - 1)

        @block.tensor
        def _(pe):
            def transposes(n):
                pe.wait_ge(h_ready, n + 1)
                for k in range(KD):
                    last = pe.transpose(tr_ps[:, k * P:(k + 1) * P], h_sb[:, k * P:(k + 1) * P], ident[:, :])
                last.then_inc(transposed, 1)
                pe.wait_ge(hT_ready, n + 1)

            pe.wait_ge(consts, 8)
            pe.wait_ge(weights_in, 16 * (4 + 2 * KD))
            pe.transpose(comb_ps[:, 0:EX * KD], b1_rows[:, :], ident[0:EX * KD, 0:EX * KD]).then_inc(small_T, 1)
            for k in range(KD):
                last = pe.transpose(root_ps[:, k * EX:(k + 1) * EX], rw_rows[:, k * P:(k + 1) * P],
                                    ident[0:EX, 0:EX])
            last.then_inc(small_T, 1)
            pe.wait_ge(counted, 1)
            pe.matmul(y_ps[0][:, 0:BLOCKS - 1], ones[:, :], below_n[:, :], start=True, stop=True)
            pe.matmul(y_ps[1][0:BLOCKS - 1, 0:1], below_n[:, :], ones[:, 0:1], start=True, stop=True) \
                .then_inc(totals, 1)
            pe.wait_ge(bounds_ok, 1)
            pe.wait_ge(tiles_ok, GROUP)
            pe.wait_ge(edges_f, 2)
            for c in range(2 * CH):
                if c >= 2:
                    pe.wait_ge(prep_out, c - 1)
                if c >= CH:
                    pe.wait_ge(shifted, c - CH + 1)
                what = idx_f[:, c, :] if c < CH else dst_loc[:, c - CH, :]
                pe.transpose(y_ps[c % 2][:, 0:P], what, ident[:, :]).then_inc(prep_T, 1)
            pe.wait_ge(shifted, CH + 1)
            pe.wait_ge(prep_out, 2 * CH - 1)
            for g in range(GROUP):
                last = pe.transpose(y_ps[0][:, g * (BLOCKS - 1):(g + 1) * (BLOCKS - 1)], dst_first[:, g, :],
                                    ident[0:BLOCKS - 1, 0:BLOCKS - 1])
            last.then_inc(prep_T, 1)
            pe.wait_ge(prep_out, 2 * CH + 1)
            pe.wait_ge(small_out, 2)

            def post_table(phase, b):
                n = n_of(phase, b)
                transposes(n)
                for c in range(CHUNKS):
                    pe.wait_ge(resid, CHUNKS * n + c + 1)
                    for k in range(KD):
                        last = pe.matmul(y_ps[c][:, :], hT[:, k, :], gnn_w_sb[:, k, 2 * c:2 * c + 2, :]
                                         .rearrange("p r e -> p (r e)"), start=(k == 0), stop=(k == KD - 1))
                    last.then_inc(y_ready, 1)
                pe.wait_ge(root_taken, n + 1)
                for k in range(KD):
                    last = pe.matmul(root_ps[:, 0:D], hT[:, k, :], gnn_w_sb[:, k, R, :],
                                     start=(k == 0), stop=(k == KD - 1))
                last.then_inc(root_ready, 1)

            def add_group(hots, rows, opens=False):
                for u in range(GROUP):
                    pe.matmul(agg_ps[:, :], hots(u), rows(u * ROW, 2 * D), start=(opens and u == 0), stop=False)
                    last = pe.matmul(agg_ps[:, 0:D], hots(u), rows(u * ROW + 2 * D, D), start=False, stop=False)
                return last

            def sum_block(phase, b):
                layer = phase - 1
                GROUP_SLOTS = SLOTS // GROUP

                def walk(g, opens=False):
                    pe.wait_ge(tile_ready, layer * TILES_P + GROUP * g + GROUP)
                    pe.wait_ge(hot_ready, layer * TILES_P + GROUP * g + GROUP)
                    if isinstance(g, int):
                        add_group(lambda u: hot_ring[:, u * P:(u + 1) * P], lambda o, n: gathered[:, o:o + n], opens)
                        return
                    slot = pe.snap(g % GROUP_SLOTS)
                    g0 = pe.snap(slot * (GROUP * ROW))
                    o0 = pe.snap(slot * (GROUP * P))
                    add_group(lambda u: hot_ring[:, bass.ds(o0 + u * P, P)],
                              lambda o, n: gathered[:, bass.ds(g0 + o, n)]).then_inc(tile_free, GROUP)

                if isinstance(b, int):
                    hi = pe.value_load(bounds[0:1, 1:2], min_val=0, max_val=GROUPS - 1)
                    walk(0, True)
                    with pe.If(hi > 0):
                        with pe.Fori(1, hi + 1) as g:
                            walk(g)
                else:
                    lo = pe.value_load(bounds[0:1, bass.ds(b, 1)], min_val=0, max_val=GROUPS - 1)
                    hi = pe.value_load(bounds[0:1, bass.ds(b + 1, 1)], min_val=0, max_val=GROUPS - 1)
                    if phase < 3:
                        pe.wait_ge(h_ready, n_of(phase, b))
                    else:
                        pe.wait_ge(z_ready, b)
                    pe.wait_ge(shared_ready, layer * BLOCKS + b)
                    g0 = pe.snap((lo % GROUP_SLOTS) * (GROUP * ROW))
                    add_group(lambda u: shared_hot[:, u * P:(u + 1) * P],
                              lambda o, n: gathered[:, bass.ds(g0 + o, n)], True)
                    with pe.If(hi > lo):
                        with pe.Fori(lo + 1, hi + 1) as g:
                            walk(g)
                pe.matmul(agg_ps[:, :], zeros[:, 0:P], zeros[:, :], start=False, stop=True).then_inc(agg_done, 1)

            def experts(b):
                transposes(n_of(3, b))
                for k in range(KD):
                    last = pe.matmul(root_ps[:, 0:EX], hT[:, k, :], rw_sb[:, k, :], start=(k == 0), stop=(k == KD - 1))
                last.then_inc(logits, 1)

                def hidden(e):
                    pe.wait_ge(gelu_done, EX * b + e + 1)
                    for f in range(KD):
                        for k in range(KD):
                            last = pe.matmul(y_ps[e % 2][:, f * P:(f + 1) * P],
                                             w1_sb[:, e, k, f * P:(f + 1) * P], hT[:, k, :],
                                             start=(k == 0), stop=(k == KD - 1))
                    last.then_inc(hid_ready, 1)

                def second_product(e):
                    pe.wait_ge(gelu_done, 2 + EX * b + e + 1)
                    if e < 2:
                        pe.wait_ge(comb_ok, b + 1)
                    pe.wait_ge(acc_ready, (1 + EX) * b + 1 + max(e - 1, 0))
                    for f in range(KD):
                        last = pe.matmul(y_ps[2 + e % 2][:, 0:D], hidden_sb[e % 2][:, f, :], w2_sb[:, e, f, :],
                                         start=(f == 0), stop=(f == KD - 1))
                    last.then_inc(exp_ready, 1)

                hidden(0)
                hidden(1)
                pe.wait_ge(comb_ok, b + 1)
                pe.transpose(comb_ps[0:EX, 0:P], comb[:, :], ident[:, :]).then_inc(combT_ps, 1)
                for e in range(EX):
                    second_product(e)
                    if e + 2 < EX:
                        hidden(e + 2)
                pe.wait_ge(combT_ok, b + 1)
                pe.matmul(root_ps[:, 0:D], combT[:, :], b2_sb[:, :], start=True, stop=True).then_inc(b2_ready, 1)

            for phase in range(4):
                if phase == 0:
                    pe.wait_ge(layer_w_in, 16 * 2 * KD)
                    with pe.Fori(0, BLOCKS) as b:
                        post_table(0, b)
                    continue
                post = experts if phase == 3 else (lambda b, phase=phase: post_table(phase, b))
                sum_block(phase, 0)
                if phase < 3:
                    pe.wait_ge(layer_w_in, 16 * 2 * KD * (phase + 1))
                with pe.Fori(1, BLOCKS) as b:
                    sum_block(phase, b)
                    post(b - 1)
                post(BLOCKS - 1)
                pe.matmul(agg_ps[:, :], zeros[:, 0:P], zeros[:, :], start=True, stop=True) \
                    .then_inc(tile_free, TILES_P - GROUP * (GROUPS - 1))


_INS = ["x", "src", "dst", "edge_type_8", "L0_gnn_weights", "L0_gnn_roots", "L0_gnn_biases", "L0_ffn_router_w",
        "L0_ffn_w1", "L0_ffn_b1", "L0_ffn_w2", "L0_ffn_b2"]


def kernel(**inputs):
    import numpy as _np
    import concourse.bacc as _bacc
    from concourse.bass_utils import run_bass_kernel_spmd as _run

    nc = _bacc.Bacc("TRN2", target_bir_lowering=False, num_devices=1)
    arrays, args = {}, []
    for name in _INS:
        a = _np.ascontiguousarray(inputs[name])
        arrays[f"in_{name}_dram"] = a
        args.append(nc.dram_tensor(f"in_{name}_dram", a.shape, mybir.dt.from_np(a.dtype), kind="ExternalInput").ap())
    out = nc.dram_tensor("out_dram", inputs["x"].shape, F32, kind="ExternalOutput").ap()
    gnn_moe(nc, *args, out)
    r = _run(nc, [arrays], core_ids=[0])
    return r.results[0]["out_dram"]
```

```python
from contextlib import ExitStack

import concourse.bass as bass
from concourse import mybir

ALU = mybir.AluOpType
ACT = mybir.ActivationFunctionType
AX = mybir.AxisListType
F32 = mybir.dt.float32
BF16 = mybir.dt.bfloat16
I32 = mybir.dt.int32
U32 = mybir.dt.uint32

P = 128
GROUP = 3
BATCH = 9
RING = 3
GROUPS_BEFORE_ROUTE = 5
GROUPS_IN_RING = RING * BATCH // GROUP
SLOTS = BATCH * RING
PARTS = 3
EPS = 1e-5


def round_up(n, m):
    return -(-n // m) * m


class Count:

    def __init__(self):
        self.base, self.k = 0, 0

    def turn(self, base):
        self.base, self.k = base, 0

    def next(self):
        self.k += 1
        return self.base + self.k


def gnn_moe(nc, x, src, dst, etype, gnn_w, gnn_root, gnn_bias, router_w, w1, b1, w2, b2, out):
    N, D = x.shape
    E = src.shape[0]
    LAYERS, R = gnn_w.shape[0], gnn_w.shape[1]
    EX = w1.shape[0]
    assert D == 256 and R == 8 and LAYERS == 3 and EX == 8
    KD = D // P
    BLOCKS = -(-N // P)
    LAST = N - (BLOCKS - 1) * P
    TILES = -(-E // P)
    GROUPS = -(-TILES // GROUP)
    FULL_GROUPS = E // (GROUP * P)
    STAGE = SLOTS
    HALVES = round_up(TILES, 2 * STAGE) // STAGE
    TILES_P = round_up(TILES, 2 * STAGE)
    CH = -(-TILES_P // P)
    CG = -(-GROUPS // P)
    NQ = TILES_P // BATCH
    PAD_NODE = BLOCKS * P
    CHUNKS = R * D // 512
    ROW = PARTS * D
    HALF = R // 2 * ROW
    PAIRS = (BLOCKS - 3) // 2
    HOT_SLOTS = 7
    HOTS_OF = (range(0, 4), range(4, HOT_SLOTS))
    LAST_HOTS = NQ - HOT_SLOTS * (PAIRS + 1)
    assert BLOCKS % 2 == 1 and 0 < LAST_HOTS <= HOT_SLOTS

    ctx = ExitStack()
    with ctx:
        def sb(name, shape, dt, where=ctx):
            return where.enter_context(nc.sbuf_tensor(name, shape, dt))

        def bank(name):
            return ctx.enter_context(nc.psum_tensor(name, [P, 512], F32))

        def sem(name):
            return ctx.enter_context(nc.semaphore(name))

        tables = [nc.dram_tensor(f"table{i}", [BLOCKS, P, R * ROW], BF16).ap() for i in range(2)]
        onehots = nc.dram_tensor("onehots", [NQ, P, BATCH * P], BF16).ap()
        dst_rows = nc.dram_tensor("dst_rows", [CH * P, P], F32).ap()

        ident = sb("ident", [P, P], F32)
        zeros = sb("zeros", [P, 2 * D], BF16)
        gnn_w_sb = sb("gnn_w_sb", [P, KD, R + 1, D], F32)
        bias_sb = sb("bias_sb", [P, LAYERS, D], F32)
        w1_sb = sb("w1_sb", [P, EX, KD, D], F32)
        w2_sb = sb("w2_sb", [P, EX, KD, D], F32)
        b1_rows = sb("b1_rows", [EX * KD, P], F32)
        b1_sb = sb("b1_sb", [P, EX * KD], F32)
        b2_sb = sb("b2_sb", [EX, D], F32)
        rw_rows = sb("rw_rows", [EX, D], F32)
        rw_sb = sb("rw_sb", [P, KD, EX], F32)
        root_sb = sb("root_sb", [P, BLOCKS * D], F32)
        idx_all = sb("idx_all", [P, CH * P], U32)
        stage_idx = sb("stage_idx", [P, 2 * STAGE], U32)
        hot_ring = sb("hot_ring", [P, SLOTS * P], BF16)
        shared_hot = sb("shared_hot", [P, GROUP * P], BF16)
        loc_shared = sb("loc_shared", [P, BLOCKS * GROUP], BF16)
        mids = sb("mids", [1, BLOCKS], I32)
        mids_f = sb("mids_f", [1, BLOCKS], F32)
        first_f = sb("first_f", [1, BLOCKS], F32)
        bounds = sb("bounds", [1, BLOCKS + 1], I32)
        x_sb = sb("x_sb", [P, D], F32)
        h_sb = sb("h_sb", [P, D], F32)
        hT = sb("hT", [P, KD, P], F32)
        residual = [sb(f"residual{i}", [P, 2, D], F32) for i in range(CHUNKS)]
        rows_out = [sb(f"rows_out{i}", [P, R // 2, PARTS, D], BF16) for i in range(2)]
        stats = sb("stats", [P, 6], F32)
        meanvar = sb("meanvar", [P, 2], F32)
        var_eps = sb("var_eps", [P, 1], F32)
        std = sb("std", [P, 1], F32)
        rstd = sb("rstd", [P, 1], F32)
        z_sb = sb("z_sb", [P, D], F32)
        sig_sb = sb("sig_sb", [P, D], F32)
        x1_sb = sb("x1_sb", [P, D], F32)
        acc_sb = sb("acc_sb", [P, D], F32)
        out_sb = sb("out_sb", [P, D], F32)
        hidden_sb = [sb(f"hidden_sb{i}", [P, KD, P], F32) for i in range(2)]
        combT = sb("combT", [EX, P], F32)
        desc8 = sb("desc8", [P, EX], F32)
        lmax = sb("lmax", [P, 1], F32)
        nlmax = sb("nlmax", [P, 1], F32)
        pexp = sb("pexp", [P, EX], F32)
        psum_e = sb("psum_e", [P, 1], F32)
        rpsum = sb("rpsum", [P, 1], F32)
        probs = sb("probs", [P, EX], F32)
        top = sb("top", [P, 2], F32)
        key = sb("key", [P, EX], F32)
        kmax = sb("kmax", [P, 1], F32)
        first = sb("first", [P, EX], F32)
        rest = sb("rest", [P, EX], F32)
        second = sb("second", [P, EX], F32)
        chosen = sb("chosen", [P, EX], F32)
        tsum = sb("tsum", [P, 1], F32)
        rtsum = sb("rtsum", [P, 1], F32)
        comb = sb("comb", [P, EX], F32)

        prep = ExitStack()
        dst_i = sb("dst_i", [P, CH, P], I32, prep)
        src_i = sb("src_i", [P, CH, P], I32, prep)
        typ_i = sb("typ_i", [P, CH, P], I32, prep)
        dst_f = sb("dst_f", [P, CH, P], F32, prep)
        idx_f = sb("idx_f", [P, CH, P], F32, prep)
        dst_loc = sb("dst_loc", [P, CH, P], F32, prep)
        dst_first = sb("dst_first", [BLOCKS - 1, GROUP, P], F32, prep)
        prep.close()
        assert (6 * CH + GROUP) * P * 4 <= SLOTS * ROW * 2
        phase0 = ExitStack()
        rows_out0 = [[sb(f"rows_out0_{q}{i}", [P, R // 2, PARTS, D], BF16, phase0) for i in range(2)]
                     for q in range(2)]
        hots0 = [sb(f"hots0_{k}", [P, BATCH, P], BF16, phase0) for k in range(HOT_SLOTS)]
        phase0.close()
        assert 4 * HALF + HOT_SLOTS * BATCH * P <= SLOTS * ROW
        gathered = sb("gathered", [P, SLOTS * ROW], BF16)
        x_bufs, h_bufs, hT_bufs = [x_sb, z_sb], [h_sb, sig_sb], [hT, hidden_sb[0]]
        ones = sb("ones", [P, P], F32)
        loc_all = sb("loc_all", [P, CH * P], BF16)
        iota_i = sb("iota_i", [P, P], I32)
        iota_b = sb("iota_b", [P, P], BF16)
        block_i = sb("block_i", [P, BLOCKS - 1], I32)
        block_f = sb("block_f", [P, BLOCKS - 1], F32)
        thresh = sb("thresh", [P, BLOCKS - 1], F32)
        last_i = sb("last_i", [P, CG, 2], I32)
        last_f = sb("last_f", [P, CG], F32)
        below = sb("below", [P, BLOCKS - 1, CG], F32)
        below_n = sb("below_n", [P, BLOCKS - 1], F32)
        start_f = sb("start_f", [P, BLOCKS - 1], F32)
        tile_i = sb("tile_i", [P, CH], I32)
        tile_f = sb("tile_f", [P, CH], F32)
        node0_i = sb("node0_i", [P, 1], I32)
        node0_f = sb("node0_f", [P, 1], F32)
        reached = sb("reached", [P, CH, BLOCKS - 1], F32)
        block_of = sb("block_of", [P, CH], F32)
        first_tiles = sb("first_tiles", [BLOCKS - 1, GROUP], U32)
        shift = sb("shift", [P, CH], F32)

        agg_ps = bank("agg_ps")
        tr_ps = bank("tr_ps")
        y_ps = [bank(f"y_ps{i}") for i in range(CHUNKS)]
        root_ps = bank("root_ps")
        comb_ps = bank("comb_ps")

        padded = sem("padded")
        edges_in = sem("edges_in")
        ends_in = sem("ends_in")
        bias_in = sem("bias_in")
        weights_in = sem("weights_in")
        layer_w_in = sem("layer_w_in")
        consts = sem("consts")
        dve_own = sem("dve_own")
        edges_f = sem("edges_f")
        counted = sem("counted")
        totals = sem("totals")
        bounds_ok = sem("bounds_ok")
        tiles_ok = sem("tiles_ok")
        dst_saved = sem("dst_saved")
        dst_got = sem("dst_got")
        shifted = sem("shifted")
        prep_T = sem("prep_T")
        prep_out = sem("prep_out")
        hot_made = sem("hot_made")
        hot_saved = [sem(f"hot_saved{k}") for k in range(HOT_SLOTS)]
        rows0_saved = [[sem(f"rows0_saved{q}{i}") for i in range(2)] for q in range(2)]
        small_T = sem("small_T")
        small_out = sem("small_out")
        x_in0 = [sem(f"x_in0{q}") for q in range(2)]
        x_in = sem("x_in")
        apart = sem("apart")
        var_ready = sem("var_ready")
        std_ready = sem("std_ready")
        h_ready = sem("h_ready")
        transposed = sem("transposed")
        hT_ready = sem("hT_ready")
        y_ready = sem("y_ready")
        part0 = sem("part0")
        resid = sem("resid")
        part1 = sem("part1")
        part2 = sem("part2")
        rows_saved = [sem(f"rows_saved{i}") for i in range(2)]
        root_ready = sem("root_ready")
        root_taken = sem("root_taken")
        staged = [sem(f"staged{s}") for s in range(2)]
        tile_in = [sem(f"tile_in{j}") for j in range(GROUPS_IN_RING)]
        tile_ready = sem("tile_ready")
        tile_free = sem("tile_free")
        hot_in = [sem(f"hot_in{j}") for j in range(RING)]
        shared_ready = sem("shared_ready")
        half_sum = sem("half_sum")
        agg_done = sem("agg_done")
        z_ready = sem("z_ready")
        sig_ready = sem("sig_ready")
        x1_ready = sem("x1_ready")
        acc_ready = sem("acc_ready")
        logits = sem("logits")
        lmax_ok = sem("lmax_ok")
        pexp_ok = sem("pexp_ok")
        comb_ok = sem("comb_ok")
        combT_ps = sem("combT_ps")
        combT_ok = sem("combT_ok")
        hid_ready = sem("hid_ready")
        gelu_done = sem("gelu_done")
        exp_ready = sem("exp_ready")
        b2_ready = sem("b2_ready")
        out_ready = sem("out_ready")
        out_free = sem("out_free")
        out_saved = sem("out_saved")

        def n_of(phase, b):
            return phase * BLOCKS + b

        def relu_rows(t):
            return t.rearrange("b p (r c) -> (b p r) c", r=R)

        def last_blocks():
            n = HOT_SLOTS * PAIRS
            for b, ks in ((BLOCKS - 3, HOTS_OF[0]), (BLOCKS - 2, HOTS_OF[1]), (BLOCKS - 1, range(LAST_HOTS))):
                yield b, ks, n
                n += HOT_SLOTS if b == BLOCKS - 2 else 0

        block = ctx.enter_context(nc.Block())

        @block.sync
        def _(sp):
            full = E // (P * P)
            rows = (E - full * P * P) // P
            tail = E - full * P * P - rows * P
            sp.wait_ge(padded, 4)
            for a, t in ((dst, dst_i), (src, src_i), (etype, typ_i)):
                sp.dma_start(t[:, 0:full, :], a[0:full * P * P].rearrange("(c p e) -> p c e", p=P, e=P)) \
                    .then_inc(edges_in, 16)
                if rows:
                    sp.dma_start(t[0:rows, full, :], a[full * P * P:full * P * P + rows * P]
                                 .rearrange("(p e) -> p e", e=P)).then_inc(edges_in, 16)
                if tail:
                    sp.dma_start(t[rows:rows + 1, full, 0:tail], a[E - tail:E].rearrange("(a e) -> a e", a=1)) \
                        .then_inc(edges_in, 16)

            def layer_weights(layer):
                for k in range(KD):
                    sp.dma_start(gnn_w_sb[:, k, 0:R, :], gnn_w[layer, :, k * P:(k + 1) * P, :]
                                 .rearrange("r p e -> p r e")).then_inc(layer_w_in, 16)
                    sp.dma_start(gnn_w_sb[:, k, R, :], gnn_root[layer, k * P:(k + 1) * P, :]) \
                        .then_inc(layer_w_in, 16)

            ends = dst[0:FULL_GROUPS * GROUP * P].rearrange("(g w) -> g w", w=GROUP * P)[:, GROUP * P - 2:]
            sp.dma_start(last_i[:, 0:FULL_GROUPS // P, :],
                         ends[0:FULL_GROUPS // P * P].rearrange("(c p) w -> p c w", p=P)).then_inc(ends_in, 16)
            sp.dma_start(last_i[0:FULL_GROUPS % P, FULL_GROUPS // P, :], ends[FULL_GROUPS // P * P:FULL_GROUPS]) \
                .then_inc(ends_in, 16)

            sp.dma_start(x_bufs[0][:, :], x[0:P, :]).then_inc(x_in0[0], 16)
            sp.dma_start(x_bufs[1][:, :], x[P:2 * P, :]).then_inc(x_in0[1], 16)
            sp.wait_ge(edges_f, 1)
            sp.dma_start(dst_rows.rearrange("(c p) e -> p c e", p=P), dst_f[:, :, :]).then_inc(dst_saved, 16)

            layer_weights(0)
            sp.dma_start(bias_sb[:, :, :], gnn_bias.rearrange("(a l) d -> a l d", a=1).broadcast_to([P, LAYERS, D])) \
                .then_inc(bias_in, 16)
            sp.dma_start(b1_rows[:, :], b1.rearrange("e (k p) -> (e k) p", p=P)).then_inc(weights_in, 16)
            sp.dma_start(rw_rows[:, :], router_w).then_inc(weights_in, 16)
            sp.dma_start(b2_sb[:, :], b2).then_inc(weights_in, 16)
            for k in range(KD):
                sp.dma_start(w1_sb[:, :, k, :], w1[:, k * P:(k + 1) * P, :].rearrange("e p f -> p e f")) \
                    .then_inc(weights_in, 16)
                sp.dma_start(w2_sb[:, :, k, :], w2[:, k * P:(k + 1) * P, :].rearrange("e p f -> p e f")) \
                    .then_inc(weights_in, 16)

            def load_x(b, q):
                sp.wait_ge(h_ready, b - 1)
                if isinstance(b, int) and b == BLOCKS - 1:
                    sp.dma_start(x_bufs[q][0:LAST, :], x[(BLOCKS - 1) * P:N, :]).then_inc(x_in0[q], 16)
                elif isinstance(b, int):
                    sp.dma_start(x_bufs[q][:, :], x[b * P:(b + 1) * P, :]).then_inc(x_in0[q], 16)
                else:
                    sp.dma_start(x_bufs[q][:, :], x[bass.ds(b * P, P), :]).then_inc(x_in0[q], 16)

            def save_hot(n, k):
                sp.wait_ge(hot_made, n + 1)
                to = onehots[n] if isinstance(n, int) else onehots[bass.ds(n, 1)].rearrange("a p e -> (a p) e")
                sp.dma_start(to, hots0[k][:, :, :].rearrange("p u e -> p (u e)")).then_inc(hot_saved[k], 16)

            def save_rows(b, q, half):
                sp.wait_ge(part2, CHUNKS + CHUNKS * b + 2 * half + 2)
                to = tables[0][b] if isinstance(b, int) else \
                    tables[0][bass.ds(b, 1)].rearrange("a p e -> (a p) e")
                sp.dma_start(to[:, half * HALF:(half + 1) * HALF],
                             rows_out0[q][half][:, :, :, :].rearrange("p r c e -> p (r c e)")) \
                    .then_inc(rows0_saved[q][half], 16)

            def save_block(b, q, ks, n):
                for k in ks:
                    save_hot(n + k, k)
                    if k == ks[1]:
                        save_rows(b, q, 0)
                save_rows(b, q, 1)

            load_x(2, 0)
            with sp.Fori(0, PAIRS - 1) as i:
                for q in range(2):
                    load_x(2 * i + q + 3, 1 - q)
                    save_block(2 * i + q, q, HOTS_OF[q], HOT_SLOTS * i)
            for q in range(2):
                load_x(BLOCKS - 2 + q, 1 - q)
                save_block(BLOCKS - 5 + q, q, HOTS_OF[q], HOT_SLOTS * (PAIRS - 1))
            for b, ks, n in last_blocks():
                save_block(b, b % 2, ks, n)

            sp.wait_ge(prep_out, 2 * CH + 1)
            for k in range(HOT_SLOTS):
                sp.wait_ge(hot_saved[k], 16 * (1 + PAIRS + 1 + (k < LAST_HOTS)))
            for layer in range(LAYERS):
                def issue(q, j):
                    sp.wait_ge(tile_free, layer * TILES_P + BATCH * q + BATCH)
                    src_ap = onehots[q] if isinstance(q, int) else onehots[bass.ds(q, 1)].rearrange("a p e -> (a p) e")
                    sp.dma_start(hot_ring[:, j * BATCH * P:(j + 1) * BATCH * P], src_ap).then_inc(hot_in[j], 16)

                def stage(half, s):
                    if isinstance(half, int):
                        sp.dma_start(stage_idx[:, s * STAGE:(s + 1) * STAGE],
                                     idx_all[:, half * STAGE:(half + 1) * STAGE]).then_inc(staged[s], 16)
                    else:
                        sp.dma_start(stage_idx[:, s * STAGE:(s + 1) * STAGE],
                                     idx_all[:, bass.ds(half * STAGE, STAGE)]).then_inc(staged[s], 16)

                def turn(i, s):
                    issue(RING * i, 0)
                    if not (isinstance(i, int) and i == HALVES - 1):
                        sp.wait_ge(tile_ready, layer * TILES_P + STAGE * i)
                        stage(i + 1, 1 - s)
                    for j in range(1, RING):
                        issue(RING * i + j, j)

                if layer > 0:
                    sp.wait_ge(tile_ready, layer * TILES_P)
                for s in range(2):
                    stage(s, s)
                for j in range(RING):
                    issue(j, j)
                if layer + 1 < LAYERS:
                    sp.wait_ge(root_ready, (layer + 1) * BLOCKS)
                    sp.wait_ge(tile_ready, layer * TILES_P + GROUP)
                    layer_weights(layer + 1)
                with sp.Fori(0, HALVES // 2 - 1) as i:
                    turn(2 * i + 1, 1)
                    turn(2 * i + 2, 0)
                turn(HALVES - 1, 1)

        @block.gpsimd
        def _(pool):
            pool.memset(ident[:, :], 0.0).then_inc(consts, 1)
            pool.wait_ge(consts, 1)
            pool.affine_select(out=ident[:, :], in_=ident[:, :], compare_op=ALU.not_equal, fill=1.0,
                               base=0, pattern=[[-1, P]], channel_multiplier=1).then_inc(consts, 1)
            pool.iota(iota_i[:, :], pattern=[[1, P]], base=0, channel_multiplier=0).then_inc(consts, 1)
            pool.iota(block_i[:, :], pattern=[[1, BLOCKS - 1]], base=1, channel_multiplier=0).then_inc(consts, 1)
            pool.iota(tile_i[:, :], pattern=[[P, CH]], base=0, channel_multiplier=1).then_inc(consts, 1)
            pool.iota(node0_i[:, :], pattern=[[0, 1]], base=P, channel_multiplier=P).then_inc(consts, 1)
            pool.memset(ones[:, :], 1.0).then_inc(consts, 1)
            pool.memset(zeros[:, :], 0.0).then_inc(consts, 1)

            pool.wait_ge(tiles_ok, GROUP)
            pool.wait_ge(dst_saved, 16)
            for g in range(GROUP):
                pool.indirect_dma_start(out=dst_first[:, g, :], out_offset=None, in_=dst_rows,
                                        in_offset=bass.IndirectOffsetOnAxis(ap=first_tiles[:, g:g + 1], axis=0)) \
                    .then_inc(dst_got, 16)

            def third_parts(b, q):
                for c in range(CHUNKS):
                    rows = rows_out0[q][c // 2]
                    pool.wait_ge(part1, CHUNKS * b + c + 1)
                    pool.wait_ge(resid, CHUNKS + CHUNKS * b + c + 1)
                    pool.tensor_tensor(rows[:, 2 * (c % 2):2 * (c % 2) + 2, 2, :], residual[c][:, :, :],
                                       rows[:, 2 * (c % 2):2 * (c % 2) + 2, 1, :], ALU.subtract).then_inc(part2, 1)

            with pool.Fori(0, PAIRS) as i:
                for q in range(2):
                    third_parts(2 * i + q, q)
            for b in range(2 * PAIRS, BLOCKS):
                third_parts(b, b % 2)


            for layer in range(LAYERS):
                rows_of = relu_rows(tables[layer % 2])

                def surplus(j):
                    return (HALVES - 1) * GROUPS_IN_RING + j >= GROUPS

                LAG = 2 if layer < LAYERS - 1 else 1

                def landed(turns, j):
                    if not (isinstance(turns, int) and turns == HALVES and surplus(j)):
                        pool.wait_ge(tile_in[j], 16 * GROUP * (layer * (HALVES - surplus(j)) + turns))
                    if j * GROUP % BATCH == 0:
                        pool.wait_ge(hot_in[j * GROUP // BATCH], 16 * (layer * HALVES + turns))
                    pool.sem_inc(tile_ready, GROUP)

                def half_gathers(half, s, turn, first_half=False, last_half=False):
                    pool.wait_ge(staged[s], 16 * (layer * (HALVES // 2) + turn + 1))
                    for j in range(GROUPS_IN_RING):
                        pool.wait_ge(tile_free, layer * TILES_P + STAGE * half + GROUP * (j + 1))
                        if first_half and j == 0:
                            if layer == 0:
                                for q in range(2):
                                    for part in range(2):
                                        pool.wait_ge(rows0_saved[q][part], 16 * (1 + BLOCKS // 2 + (q == 0)))
                            else:
                                pool.wait_ge(rows_saved[0], 16 * (1 + BLOCKS * layer))
                                pool.wait_ge(rows_saved[1], 16 * (1 + BLOCKS * layer))
                        pool.sem_inc(apart, 1)
                        for n in range(j * GROUP, j * GROUP if last_half and surplus(j) else (j + 1) * GROUP):
                            pool.indirect_dma_start(
                                out=gathered[:, n * ROW:(n + 1) * ROW], out_offset=None, in_=rows_of,
                                in_offset=bass.IndirectOffsetOnAxis(ap=stage_idx[:, s * STAGE + n:s * STAGE + n + 1], axis=0)) \
                                .then_inc(tile_in[j], 16)
                        if not (first_half and j < LAG):
                            landed(half if j < LAG else half + 1, (j - LAG) % GROUPS_IN_RING)

                if layer == 0:
                    pool.wait_ge(prep_out, 2 * CH + 1)
                    for k in range(HOT_SLOTS):
                        pool.wait_ge(hot_saved[k], 16 * (1 + PAIRS + 1 + (k < LAST_HOTS)))
                half_gathers(0, 0, 0, first_half=True)
                half_gathers(1, 1, 0)
                with pool.Fori(1, HALVES // 2 - 1) as i:
                    half_gathers(2 * i, 0, i)
                    half_gathers(2 * i + 1, 1, i)
                half_gathers(HALVES - 2, 0, HALVES // 2 - 1)
                half_gathers(HALVES - 1, 1, HALVES // 2 - 1, last_half=True)
                for j in range(GROUPS_IN_RING - LAG, GROUPS_IN_RING):
                    landed(HALVES, j)

        @block.scalar
        def _(act):
            def post_table(phase, b):
                n = n_of(phase, b)
                act.wait_ge(transposed, n + 1)
                act.activation(hT[:, :, :], tr_ps[:, 0:KD * P].rearrange("p (k n) -> p k n", k=KD),
                               ACT.Relu).then_inc(hT_ready, 1)

                def p0(c):
                    if c % 2 == 0:
                        act.wait_ge(rows_saved[c // 2], 16 * (1 + n_of(phase - 1, b)))
                    act.wait_ge(y_ready, CHUNKS * n + c + 1)
                    act.activation(rows_out[c // 2][:, 2 * (c % 2):2 * (c % 2) + 2, 0, :],
                                   y_ps[c][:, :].rearrange("p (r e) -> p r e", r=2), ACT.Copy).then_inc(part0, 1)

                def p1(c):
                    act.wait_ge(resid, CHUNKS + CHUNKS * n + c + 1)
                    act.activation(rows_out[c // 2][:, 2 * (c % 2):2 * (c % 2) + 2, 1, :], residual[c][:, :, :],
                                   ACT.Copy).then_inc(part1, 1)

                def save(half):
                    act.wait_ge(part2, CHUNKS + CHUNKS * n + 2 * half + 2)
                    t = tables[phase % 2]
                    to = t[b] if isinstance(b, int) else t[bass.ds(b, 1)].rearrange("a p e -> (a p) e")
                    act.dma_start(to[:, half * HALF:(half + 1) * HALF],
                                  rows_out[half][:, :, :, :].rearrange("p r c e -> p (r c e)")) \
                        .then_inc(rows_saved[half], 16)

                p0(0)
                p0(1)
                p1(0)
                p0(2)
                p1(1)
                p0(3)
                save(0)
                p1(2)
                p1(3)
                save(1)

            def root_of_variance(nth):
                act.wait_ge(var_ready, nth + 1)
                act.activation(std[:, :], var_eps[:, :], ACT.Sqrt).then_inc(std_ready, 1)

            def transposed0(b, q):
                act.wait_ge(transposed, b + 1)
                act.activation(hT_bufs[q][:, :, :], tr_ps[:, 0:KD * P].rearrange("p (k n) -> p k n", k=KD),
                               ACT.Copy).then_inc(hT_ready, 1)

            def post_table0(b, q):
                def p0(c):
                    if c % 2 == 0:
                        i = b // 2 if isinstance(b, int) else pair
                        act.wait_ge(rows0_saved[q][c // 2], 16 * (1 + i))
                    act.wait_ge(y_ready, CHUNKS * b + c + 1)
                    act.activation(rows_out0[q][c // 2][:, 2 * (c % 2):2 * (c % 2) + 2, 0, :],
                                   y_ps[c][:, :].rearrange("p (r e) -> p r e", r=2), ACT.Copy).then_inc(part0, 1)

                def p1(c):
                    act.wait_ge(resid, CHUNKS + CHUNKS * b + c + 1)
                    act.activation(rows_out0[q][c // 2][:, 2 * (c % 2):2 * (c % 2) + 2, 1, :], residual[c][:, :, :],
                                   ACT.Copy).then_inc(part1, 1)

                is_int = isinstance(b, int)
                if not (is_int and b + 1 >= BLOCKS):
                    transposed0(b + 1, 1 - q)
                p0(0)
                p0(1)
                p1(0)
                if not (is_int and b + 2 >= BLOCKS):
                    root_of_variance(b + 2)
                p0(2)
                p1(1)
                p0(3)
                p1(2)
                p1(3)

            root_of_variance(0)
            transposed0(0, 0)
            root_of_variance(1)
            with act.Fori(0, PAIRS) as pair:
                for q in range(2):
                    post_table0(2 * pair + q, q)
            for b in range(2 * PAIRS, BLOCKS):
                post_table0(b, b % 2)

            act.wait_ge(small_T, 1)
            act.activation(b1_sb[:, :], comb_ps[:, 0:EX * KD], ACT.Copy).then_inc(small_out, 1)
            act.wait_ge(small_T, 2)
            act.activation(rw_sb[:, :, :], root_ps[:, 0:KD * EX].rearrange("p (k e) -> p k e", k=KD), ACT.Copy) \
                .then_inc(small_out, 1)

            for phase in (1, 2):
                with act.Fori(0, BLOCKS) as b:
                    post_table(phase, b)

            def load_x(b):
                if isinstance(b, int) and b == BLOCKS - 1:
                    act.dma_start(x_sb[0:LAST, :], x[(BLOCKS - 1) * P:N, :]).then_inc(x_in, 16)
                elif isinstance(b, int):
                    act.dma_start(x_sb[:, :], x[b * P:(b + 1) * P, :]).then_inc(x_in, 16)
                else:
                    act.dma_start(x_sb[:, :], x[bass.ds(b * P, P), :]).then_inc(x_in, 16)

            def sigmoid(b):
                act.wait_ge(z_ready, b + 1)
                act.activation(sig_sb[:, :], z_sb[:, :], ACT.Sigmoid).then_inc(sig_ready, 1)

            def experts(b, last_block=False):
                n = n_of(3, b)
                act.wait_ge(transposed, n + 1)
                act.activation(hT[:, :, :], tr_ps[:, 0:KD * P].rearrange("p (k n) -> p k n", k=KD), ACT.Copy) \
                    .then_inc(hT_ready, 1)
                act.wait_ge(lmax_ok, b + 1)
                act.activation(pexp[:, :], root_ps[:, 0:EX], ACT.Exp, bias=nlmax[:, 0:1],
                               accum_out=psum_e[:, 0:1]).then_inc(pexp_ok, 1)
                for e in range(EX):
                    act.wait_ge(hid_ready, EX * b + e + 1)
                    for f in range(KD):
                        last = act.activation(hidden_sb[e % 2][:, f, :], y_ps[e % 2][:, f * P:(f + 1) * P],
                                              ACT.Gelu, bias=b1_sb[:, e * KD + f:e * KD + f + 1])
                    last.then_inc(gelu_done, 1)
                    if e == 3:
                        act.wait_ge(combT_ps, b + 1)
                        act.activation(combT[:, :], comb_ps[0:EX, 0:P], ACT.Copy).then_inc(combT_ok, 1)
                act.wait_ge(out_ready, b + 1)
                if last_block:
                    act.dma_start(out[(BLOCKS - 1) * P:N, :], out_sb[0:LAST, :]).then_inc(out_saved, 16)
                else:
                    act.dma_start(out[bass.ds(b * P, P), :], out_sb[:, :]).then_inc(out_saved, 16)

            load_x(0)
            sigmoid(0)
            act.wait_ge(x1_ready, 1)
            load_x(1)
            root_of_variance(BLOCKS)
            with act.Fori(1, BLOCKS - 2) as b:
                experts(b - 1)
                sigmoid(b)
                act.wait_ge(x1_ready, b + 1)
                load_x(b + 1)
                root_of_variance(BLOCKS + b)
                act.wait_ge(out_saved, 16 * b)
                act.sem_inc(out_free, 1)
            experts(BLOCKS - 3)
            sigmoid(BLOCKS - 2)
            act.wait_ge(x1_ready, BLOCKS - 1)
            load_x(BLOCKS - 1)
            root_of_variance(2 * BLOCKS - 2)
            act.wait_ge(out_saved, 16 * (BLOCKS - 2))
            act.sem_inc(out_free, 1)
            experts(BLOCKS - 2)
            sigmoid(BLOCKS - 1)
            root_of_variance(2 * BLOCKS - 1)
            act.wait_ge(out_saved, 16 * (BLOCKS - 1))
            act.sem_inc(out_free, 1)
            experts(BLOCKS - 1, True)
            act.wait_ge(out_saved, 16 * BLOCKS)

        @block.vector
        def _(dve):
            own = Count()
            full = E // (P * P)
            dve.memset(dst_i[:, full:CH, :], PAD_NODE).then_inc(padded, 1)
            dve.memset(src_i[:, full:CH, :], 0).then_inc(padded, 1)
            dve.memset(typ_i[:, full:CH, :], 0).then_inc(padded, 1)
            dve.memset(last_i[:, :, :], PAD_NODE).then_inc(padded, 1)
            dve.memset(loc_shared[:, :], -1.0).then_inc(dve_own, 1)
            dve.wait_ge(dve_own, own.next())
            dve.sem_inc(resid, CHUNKS)
            dve.sem_inc(part2, CHUNKS)
            for one in (*rows_saved, *rows0_saved[0], *rows0_saved[1], *hot_saved):
                dve.sem_inc(one, 16)
            dve.sem_inc(root_taken, 1)
            dve.sem_inc(tile_free, SLOTS)
            dve.sem_inc(gelu_done, 2)
            dve.sem_inc(out_free, 1)

            n_loads = 1 + ((E - full * P * P) // P > 0) + (E % P > 0)
            dve.wait_ge(edges_in, 16 * 3 * n_loads)
            dve.tensor_copy(dst_f[:, :, :], dst_i[:, :, :]).then_inc(edges_f, 1)
            dve.scalar_tensor_tensor(out=idx_f[:, :, :], in0=src_i[:, :, :], scalar=float(R), in1=typ_i[:, :, :],
                                     op0=ALU.mult, op1=ALU.add).then_inc(edges_f, 1)
            dve.wait_ge(consts, 8)
            dve.tensor_copy(iota_b[:, :], iota_i[:, :]).then_inc(dve_own, 1)
            dve.wait_ge(dve_own, own.next())
            dve.tensor_copy(block_f[:, :], block_i[:, :]).then_inc(dve_own, 1)
            dve.wait_ge(dve_own, own.next())
            dve.tensor_scalar(thresh[:, :], block_f[:, :], float(P), None, ALU.mult).then_inc(dve_own, 1)
            dve.wait_ge(dve_own, own.next())
            dve.tensor_copy(tile_f[:, :], tile_i[:, :]).then_inc(dve_own, 1)
            dve.wait_ge(dve_own, own.next())
            dve.tensor_copy(node0_f[:, :], node0_i[:, :]).then_inc(dve_own, 1)
            dve.wait_ge(dve_own, own.next())
            dve.wait_ge(ends_in, 16 * 2)
            dve.tensor_copy(last_f[:, :], last_i[:, :, 1]).then_inc(dve_own, 1)
            dve.wait_ge(dve_own, own.next())
            B1 = BLOCKS - 1
            dve.tensor_tensor(
                below[:, :, :], last_f[:, :].rearrange("p (b c) -> p b c", b=1).broadcast_to([P, B1, CG]),
                thresh[:, :].rearrange("p (b c) -> p b c", c=1).broadcast_to([P, B1, CG]), ALU.is_lt).then_inc(dve_own, 1)
            dve.wait_ge(dve_own, own.next())
            dve.tensor_reduce(below_n[:, :], below[:, :, :], AX.X, ALU.add).then_inc(counted, 1)
            dve.wait_ge(totals, 1)
            for g in range(GROUP):
                dve.tensor_scalar(first_tiles[:, g:g + 1], y_ps[1][0:B1, 0:1], float(GROUP), float(g),
                                  ALU.mult, ALU.add).then_inc(tiles_ok, 1)
            dve.tensor_scalar(start_f[:, :], y_ps[0][:, 0:B1], float(GROUP), float(GROUP),
                              ALU.mult, ALU.add).then_inc(dve_own, 1)
            dve.wait_ge(dve_own, own.next())
            dve.tensor_copy(bounds[0:1, 1:BLOCKS], y_ps[0][0:1, 0:B1]).then_inc(dve_own, 1)
            dve.wait_ge(dve_own, own.next())
            dve.memset(bounds[0:1, 0:1], 0).then_inc(dve_own, 1)
            dve.wait_ge(dve_own, own.next())
            dve.memset(mids_f[0:1, 0:1], 0.0).then_inc(dve_own, 1)
            dve.wait_ge(dve_own, own.next())
            dve.memset(first_f[0:1, B1:BLOCKS], GROUPS - 1.0).then_inc(dve_own, 1)
            dve.wait_ge(dve_own, own.next())
            dve.tensor_copy(first_f[0:1, 0:B1], y_ps[0][0:1, 0:B1]).then_inc(dve_own, 1)
            dve.wait_ge(dve_own, own.next())
            dve.scalar_tensor_tensor(out=mids_f[0:1, 1:BLOCKS], in0=first_f[0:1, 0:B1],
                                     scalar=float(GROUPS_BEFORE_ROUTE), in1=first_f[0:1, 1:BLOCKS],
                                     op0=ALU.add, op1=ALU.min).then_inc(dve_own, 1)
            dve.wait_ge(dve_own, own.next())
            dve.tensor_copy(mids[:, :], mids_f[:, :]).then_inc(dve_own, 1)
            dve.wait_ge(dve_own, own.next())
            dve.memset(bounds[0:1, BLOCKS:BLOCKS + 1], GROUPS - 1).then_inc(bounds_ok, 1)
            dve.tensor_tensor(
                reached[:, :, :], start_f[:, :].rearrange("p (c b) -> p c b", c=1).broadcast_to([P, CH, B1]),
                tile_f[:, :].rearrange("p (c b) -> p c b", b=1).broadcast_to([P, CH, B1]), ALU.is_le).then_inc(dve_own, 1)
            dve.wait_ge(dve_own, own.next())
            dve.tensor_reduce(block_of[:, :], reached[:, :, :], AX.X, ALU.add).then_inc(dve_own, 1)
            dve.wait_ge(dve_own, own.next())
            dve.tensor_scalar(shift[:, :], block_of[:, :], -float(P), None, ALU.mult).then_inc(dve_own, 1)
            dve.wait_ge(dve_own, own.next())
            for c in range(CH):
                dve.tensor_scalar(dst_loc[:, c, :], dst_f[:, c, :], shift[:, c:c + 1], None, ALU.add) \
                    .then_inc(shifted, 1)
            dve.wait_ge(dst_got, 16 * GROUP)
            dve.tensor_scalar(dst_first[:, :, :], dst_first[:, :, :], node0_f[0:B1, 0:1], None, ALU.subtract) \
                .then_inc(shifted, 1)
            for c in range(CH):
                dve.wait_ge(prep_T, c + 1)
                dve.tensor_copy(idx_all[:, c * P:(c + 1) * P], y_ps[c % 2][:, 0:P]).then_inc(prep_out, 1)
            for c in range(CH):
                dve.wait_ge(prep_T, CH + c + 1)
                dve.tensor_copy(loc_all[:, c * P:(c + 1) * P], y_ps[(CH + c) % 2][:, 0:P]).then_inc(prep_out, 1)
            dve.wait_ge(prep_T, 2 * CH + 1)
            dve.tensor_copy(loc_shared[:, 0:B1 * GROUP].rearrange("p (b g) -> p b g", g=GROUP),
                            y_ps[0][:, 0:B1 * GROUP].rearrange("p (g b) -> p b g", g=GROUP)).then_inc(prep_out, 1)
            links = own.k

            LN_LINKS = 3

            def statistics(source):
                dve.bn_stats(stats[:, :], source[:, :]).then_inc(dve_own, 1)
                dve.wait_ge(dve_own, own.next())
                dve.sem_inc(apart, 1)
                dve.bn_aggr(meanvar[:, :], stats[:, :]).then_inc(dve_own, 1)
                dve.wait_ge(dve_own, own.next())
                dve.tensor_scalar(var_eps[:, :], meanvar[:, 1:2], EPS, None, ALU.add).then_inc(var_ready, 1)

            def scale(source, to, nth):
                dve.wait_ge(std_ready, nth + 1)
                dve.reciprocal(rstd[:, :], std[:, :]).then_inc(dve_own, 1)
                dve.wait_ge(dve_own, own.next())
                dve.tensor_scalar(to[:, :], source[:, :], meanvar[:, 0:1], rstd[:, 0:1],
                                  ALU.subtract, ALU.mult).then_inc(h_ready, 1)

            def layer_norm(source, nth):
                statistics(source)
                scale(source, h_sb, nth)

            def statistics0(b, q, turn):
                own.turn(links + LN_LINKS * b)
                dve.wait_ge(x_in0[q], 16 * (1 + turn))
                if not (isinstance(b, int) and b == 0):
                    dve.wait_ge(h_ready, b)
                statistics(x_bufs[q])

            def scale0(b, q):
                if not (isinstance(b, int) and b < 2):
                    dve.wait_ge(transposed, b - 1)
                scale(x_bufs[q], h_bufs[q], b)

            def post_table(phase, b):
                n = n_of(phase, b)

                def r1(c):
                    dve.wait_ge(part0, CHUNKS * n + c + 1)
                    dve.tensor_tensor(residual[c][:, :, :], y_ps[c][:, :].rearrange("p (r e) -> p r e", r=2),
                                      rows_out[c // 2][:, 2 * (c % 2):2 * (c % 2) + 2, 0, :],
                                      ALU.subtract).then_inc(resid, 1)

                def p2(c):
                    dve.wait_ge(part1, CHUNKS * n + c + 1)
                    dve.wait_ge(resid, CHUNKS + CHUNKS * n + c + 1)
                    dve.tensor_tensor(rows_out[c // 2][:, 2 * (c % 2):2 * (c % 2) + 2, 2, :],
                                      residual[c][:, :, :],
                                      rows_out[c // 2][:, 2 * (c % 2):2 * (c % 2) + 2, 1, :],
                                      ALU.subtract).then_inc(part2, 1)

                dve.wait_ge(root_taken, n + 1)
                r1(0)
                r1(1)
                p2(0)
                r1(2)
                p2(1)
                r1(3)
                p2(2)
                p2(3)
                dve.wait_ge(root_ready, n + 1)
                to = root_sb[:, bass.ds(b * D, D)] if not isinstance(b, int) else root_sb[:, b * D:(b + 1) * D]
                dve.tensor_tensor(to, root_ps[:, 0:D], bias_sb[:, phase, :], ALU.add).then_inc(root_taken, 1)

            def take_sum(phase, b, to):
                dve.wait_ge(agg_done, (phase - 1) * BLOCKS + b + 1)
                dve.wait_ge(root_taken, 1 + (phase - 1) * BLOCKS + b + 1)
                own_term = root_sb[:, bass.ds(b * D, D)] if not isinstance(b, int) else root_sb[:, b * D:(b + 1) * D]
                dve.tensor_tensor(own_term, agg_ps[:, 0:D], own_term, ALU.add).then_inc(half_sum, 1)
                dve.wait_ge(half_sum, (phase - 1) * BLOCKS + b + 1)
                return dve.tensor_tensor(to[:, :], agg_ps[:, D:2 * D], own_term, ALU.add)

            group_bc = iota_b[:, :].rearrange("p (u e) -> p u e", u=1).broadcast_to([P, GROUP, P])

            def make_shared(b):
                loc = loc_shared[:, bass.ds((b - 1) * GROUP, GROUP)] if not isinstance(b, int) else \
                    loc_shared[:, (b - 1) * GROUP:b * GROUP]
                dve.tensor_tensor(shared_hot[:, :].rearrange("p (u e) -> p u e", u=GROUP), group_bc,
                                  loc.rearrange("p (u e) -> p u e", e=1).broadcast_to([P, GROUP, P]),
                                  ALU.is_equal).then_inc(shared_ready, 1)

            node_bc = iota_b[:, :].rearrange("p (u e) -> p u e", u=1).broadcast_to([P, BATCH, P])

            def make_hot(n, k, turn):
                dve.wait_ge(hot_saved[k], 16 * (1 + turn))
                loc = loc_all[:, n * BATCH:(n + 1) * BATCH] if isinstance(n, int) else \
                    loc_all[:, bass.ds(n * BATCH, BATCH)]
                dve.tensor_tensor(hots0[k][:, :, :], node_bc,
                                  loc.rearrange("p (u e) -> p u e", e=1).broadcast_to([P, BATCH, P]),
                                  ALU.is_equal).then_inc(hot_made, 1)

            def post_table0(b, q, ks, n, turn):
                def r1(c):
                    dve.wait_ge(part2, CHUNKS * b + c + 1)
                    dve.wait_ge(part0, CHUNKS * b + c + 1)
                    dve.tensor_tensor(residual[c][:, :, :], y_ps[c][:, :].rearrange("p (r e) -> p r e", r=2),
                                      rows_out0[q][c // 2][:, 2 * (c % 2):2 * (c % 2) + 2, 0, :],
                                      ALU.subtract).then_inc(resid, 1)

                ahead = not (isinstance(b, int) and b + 2 >= BLOCKS)
                hots = list(ks)
                r1(0)
                if ahead:
                    statistics0(b + 2, q, turn + 1)
                r1(1)
                make_hot(n + hots[0], hots[0], turn)
                r1(2)
                if ahead:
                    scale0(b + 2, q)
                make_hot(n + hots[1], hots[1], turn)
                r1(3)
                dve.wait_ge(root_ready, b + 1)
                to = root_sb[:, bass.ds(b * D, D)] if not isinstance(b, int) else root_sb[:, b * D:(b + 1) * D]
                dve.tensor_tensor(to, root_ps[:, 0:D], bias_sb[:, 0, :], ALU.add).then_inc(root_taken, 1)
                for k in hots[2:]:
                    make_hot(n + k, k, turn)

            dve.wait_ge(bias_in, 16)
            for b in range(2):
                statistics0(b, b, 0)
                scale0(b, b)
            with dve.Fori(0, PAIRS) as i:
                for q in range(2):
                    post_table0(2 * i + q, q, HOTS_OF[q], HOT_SLOTS * i, i)
            for b, ks, n in last_blocks():
                post_table0(b, b % 2, ks, n, n // HOT_SLOTS)
            links += LN_LINKS * BLOCKS

            for phase in (1, 2):
                def h_block(b):
                    if not (phase == 1 and isinstance(b, int) and b == 0):
                        dve.wait_ge(transposed, n_of(phase, b))
                    take_sum(phase, b, h_sb).then_inc(h_ready, 1)
                    make_shared(b + 1)

                h_block(0)
                with dve.Fori(1, BLOCKS - 1) as b:
                    h_block(b)
                    post_table(phase, b - 1)
                post_table(phase, BLOCKS - 2)
                h_block(BLOCKS - 1)
                post_table(phase, BLOCKS - 1)

            TOK_LINKS = LN_LINKS
            RT_LINKS = 15
            own.turn(links)
            dve.tensor_copy(desc8[:, :], iota_i[:, 0:EX]).then_inc(dve_own, 1)
            dve.wait_ge(dve_own, own.next())
            dve.tensor_scalar(desc8[:, :], desc8[:, :], -1.0, float(EX), ALU.mult, ALU.add).then_inc(dve_own, 1)
            dve.wait_ge(dve_own, own.next())
            links += 2

            def tokens(b):
                own.turn(links + (TOK_LINKS + RT_LINKS) * b)
                dve.wait_ge(sig_ready, b + 1)
                dve.wait_ge(x_in, 16 * (b + 1))
                dve.tensor_tensor(x1_sb[:, :], x_sb[:, :], sig_sb[:, :], ALU.add).then_inc(x1_ready, 1)
                dve.wait_ge(x1_ready, b + 1)
                dve.wait_ge(transposed, n_of(3, b))
                layer_norm(x1_sb, BLOCKS + b)
                dve.wait_ge(h_ready, n_of(3, b) + 1)
                dve.tensor_tensor(acc_sb[:, :], x1_sb[:, :], h_sb[:, :], ALU.add).then_inc(acc_ready, 1)

            def route(b):
                own.turn(links + (TOK_LINKS + RT_LINKS) * b + TOK_LINKS)
                dve.wait_ge(logits, b + 1)
                dve.tensor_reduce(lmax[:, :], root_ps[:, 0:EX], AX.X, ALU.max).then_inc(dve_own, 1)
                dve.wait_ge(dve_own, own.next())
                dve.tensor_scalar(nlmax[:, :], lmax[:, :], -1.0, None, ALU.mult).then_inc(lmax_ok, 1)
                dve.wait_ge(pexp_ok, b + 1)
                dve.reciprocal(rpsum[:, :], psum_e[:, :]).then_inc(dve_own, 1)
                dve.wait_ge(dve_own, own.next())
                dve.tensor_scalar(probs[:, :], pexp[:, :], rpsum[:, 0:1], None, ALU.mult).then_inc(dve_own, 1)
                dve.wait_ge(dve_own, own.next())
                dve.tensor_reduce(top[:, 0:1], probs[:, :], AX.X, ALU.max).then_inc(dve_own, 1)
                dve.wait_ge(dve_own, own.next())
                dve.scalar_tensor_tensor(out=key[:, :], in0=probs[:, :], scalar=top[:, 0:1],
                                         in1=desc8[:, :], op0=ALU.is_equal, op1=ALU.mult).then_inc(dve_own, 1)
                dve.wait_ge(dve_own, own.next())
                dve.tensor_reduce(kmax[:, :], key[:, :], AX.X, ALU.max).then_inc(dve_own, 1)
                dve.wait_ge(dve_own, own.next())
                dve.tensor_scalar(first[:, :], key[:, :], kmax[:, 0:1], None, ALU.is_equal).then_inc(dve_own, 1)
                dve.wait_ge(dve_own, own.next())
                dve.scalar_tensor_tensor(out=rest[:, :], in0=first[:, :], scalar=-2.0,
                                         in1=probs[:, :], op0=ALU.mult, op1=ALU.add).then_inc(dve_own, 1)
                dve.wait_ge(dve_own, own.next())
                dve.tensor_reduce(top[:, 1:2], rest[:, :], AX.X, ALU.max).then_inc(dve_own, 1)
                dve.wait_ge(dve_own, own.next())
                dve.scalar_tensor_tensor(out=key[:, :], in0=rest[:, :], scalar=top[:, 1:2],
                                         in1=desc8[:, :], op0=ALU.is_equal, op1=ALU.mult).then_inc(dve_own, 1)
                dve.wait_ge(dve_own, own.next())
                dve.tensor_reduce(kmax[:, :], key[:, :], AX.X, ALU.max).then_inc(dve_own, 1)
                dve.wait_ge(dve_own, own.next())
                dve.scalar_tensor_tensor(out=chosen[:, :], in0=key[:, :], scalar=kmax[:, 0:1],
                                         in1=first[:, :], op0=ALU.is_equal, op1=ALU.add).then_inc(dve_own, 1)
                dve.wait_ge(dve_own, own.next())
                dve.tensor_tensor(second[:, :], chosen[:, :], probs[:, :], ALU.mult).then_inc(dve_own, 1)
                dve.wait_ge(dve_own, own.next())
                dve.tensor_scalar(tsum[:, :], top[:, 0:1], top[:, 1:2], 1e-12, ALU.add, ALU.max).then_inc(dve_own, 1)
                dve.wait_ge(dve_own, own.next())
                dve.reciprocal(rtsum[:, :], tsum[:, :]).then_inc(dve_own, 1)
                dve.wait_ge(dve_own, own.next())
                assert own.k == RT_LINKS
                dve.tensor_scalar(comb[:, :], second[:, :], rtsum[:, 0:1], None, ALU.mult).then_inc(comb_ok, 1)

            def experts(b):
                dve.wait_ge(comb_ok, b + 1)
                for e in range(EX):
                    dve.wait_ge(acc_ready, (1 + EX) * b + 1 + e)
                    dve.wait_ge(exp_ready, EX * b + e + 1)
                    dve.scalar_tensor_tensor(out=acc_sb[:, :], in0=y_ps[2 + e % 2][:, 0:D], scalar=comb[:, e:e + 1],
                                             in1=acc_sb[:, :], op0=ALU.mult, op1=ALU.add).then_inc(acc_ready, 1)
                dve.wait_ge(acc_ready, (1 + EX) * (b + 1))
                dve.wait_ge(b2_ready, b + 1)
                dve.wait_ge(out_free, b + 1)
                dve.tensor_tensor(out_sb[:, :], acc_sb[:, :], root_ps[:, 0:D], ALU.add).then_inc(out_ready, 1)

            take_sum(3, 0, z_sb).then_inc(z_ready, 1)
            make_shared(1)
            tokens(0)
            with dve.Fori(1, BLOCKS - 1) as b:
                route(b - 1)
                take_sum(3, b, z_sb).then_inc(z_ready, 1)
                make_shared(b + 1)
                experts(b - 1)
                tokens(b)
            route(BLOCKS - 2)
            experts(BLOCKS - 2)
            take_sum(3, BLOCKS - 1, z_sb).then_inc(z_ready, 1)
            tokens(BLOCKS - 1)
            route(BLOCKS - 1)
            experts(BLOCKS - 1)

        @block.tensor
        def _(pe):
            def transpose_h(n, q=0):
                pe.wait_ge(h_ready, n + 1)
                for k in range(KD):
                    last = pe.transpose(tr_ps[:, k * P:(k + 1) * P], h_bufs[q][:, k * P:(k + 1) * P], ident[:, :])
                last.then_inc(transposed, 1)

            def transposes(n):
                transpose_h(n)
                pe.wait_ge(hT_ready, n + 1)

            pe.wait_ge(consts, 8)
            pe.wait_ge(counted, 1)
            pe.matmul(y_ps[0][:, 0:BLOCKS - 1], ones[:, :], below_n[:, :], start=True, stop=True)
            pe.matmul(y_ps[1][0:BLOCKS - 1, 0:1], below_n[:, :], ones[:, 0:1], start=True, stop=True) \
                .then_inc(totals, 1)
            pe.wait_ge(bounds_ok, 1)
            pe.wait_ge(tiles_ok, GROUP)
            pe.wait_ge(edges_f, 2)
            for c in range(2 * CH):
                if c >= 2:
                    pe.wait_ge(prep_out, c - 1)
                if c >= CH:
                    pe.wait_ge(shifted, c - CH + 1)
                what = idx_f[:, c, :] if c < CH else dst_loc[:, c - CH, :]
                pe.transpose(y_ps[c % 2][:, 0:P], what, ident[:, :]).then_inc(prep_T, 1)
            pe.wait_ge(shifted, CH + 1)
            pe.wait_ge(prep_out, 2 * CH - 1)
            for g in range(GROUP):
                last = pe.transpose(y_ps[0][:, g * (BLOCKS - 1):(g + 1) * (BLOCKS - 1)], dst_first[:, g, :],
                                    ident[0:BLOCKS - 1, 0:BLOCKS - 1])
            last.then_inc(prep_T, 1)
            pe.wait_ge(prep_out, 2 * CH + 1)

            def table_rows(n, q=0):
                for c in range(CHUNKS):
                    pe.wait_ge(resid, CHUNKS * n + c + 1)
                    for k in range(KD):
                        last = pe.matmul(y_ps[c][:, :], hT_bufs[q][:, k, :], gnn_w_sb[:, k, 2 * c:2 * c + 2, :]
                                         .rearrange("p r e -> p (r e)"), start=(k == 0), stop=(k == KD - 1))
                    last.then_inc(y_ready, 1)
                pe.wait_ge(root_taken, n + 1)
                for k in range(KD):
                    last = pe.matmul(root_ps[:, 0:D], hT_bufs[q][:, k, :], gnn_w_sb[:, k, R, :],
                                     start=(k == 0), stop=(k == KD - 1))
                last.then_inc(root_ready, 1)

            def post_table(phase, b):
                transposes(n_of(phase, b))
                table_rows(n_of(phase, b))

            def post_table0(b, q):
                pe.wait_ge(hT_ready, b + 1)
                if not (isinstance(b, int) and b + 1 >= BLOCKS):
                    transpose_h(b + 1, 1 - q)
                table_rows(b, q)

            def add_group(hots, rows, opens=False):
                for u in range(GROUP):
                    pe.matmul(agg_ps[:, :], hots(u), rows(u * ROW, 2 * D), start=(opens and u == 0), stop=False)
                    last = pe.matmul(agg_ps[:, 0:D], hots(u), rows(u * ROW + 2 * D, D), start=False, stop=False)
                return last

            def sum_block(phase, b, between=None):
                layer = phase - 1

                def walk(g, opens=False):
                    pe.wait_ge(tile_ready, layer * TILES_P + GROUP * g + GROUP)
                    if isinstance(g, int):
                        add_group(lambda u: hot_ring[:, u * P:(u + 1) * P], lambda o, n: gathered[:, o:o + n], opens)
                        return
                    slot = pe.snap(g % GROUPS_IN_RING)
                    g0 = pe.snap(slot * (GROUP * ROW))
                    o0 = pe.snap(slot * (GROUP * P))
                    add_group(lambda u: hot_ring[:, bass.ds(o0 + u * P, P)],
                              lambda o, n: gathered[:, bass.ds(g0 + o, n)]).then_inc(tile_free, GROUP)

                if isinstance(b, int) and b == 0:
                    hi = pe.value_load(bounds[0:1, 1:2], min_val=0, max_val=GROUPS - 1)
                    walk(0, True)
                    with pe.If(hi > 0):
                        with pe.Fori(1, hi + 1) as g:
                            walk(g)
                else:
                    at = bounds[0:1, b:b + 2] if isinstance(b, int) else bounds[0:1, bass.ds(b, 2)]
                    lo = pe.value_load(at[0:1, 0:1], min_val=0, max_val=GROUPS - 1)
                    hi = pe.value_load(at[0:1, 1:2], min_val=0, max_val=GROUPS - 1)
                    if phase < 3:
                        pe.wait_ge(h_ready, n_of(phase, b))
                    else:
                        pe.wait_ge(z_ready, b)
                    pe.wait_ge(shared_ready, layer * BLOCKS + b)
                    g0 = pe.snap((lo % GROUPS_IN_RING) * (GROUP * ROW))
                    add_group(lambda u: shared_hot[:, u * P:(u + 1) * P],
                              lambda o, n: gathered[:, bass.ds(g0 + o, n)], True)
                    if between is not None:
                        mid = pe.value_load(mids[0:1, bass.ds(b, 1)], min_val=0, max_val=GROUPS - 1)
                        with pe.If(mid > lo):
                            with pe.Fori(lo + 1, mid + 1) as g:
                                walk(g)
                        between()
                        lo = mid
                    with pe.If(hi > lo):
                        with pe.Fori(lo + 1, hi + 1) as g:
                            walk(g)
                pe.matmul(agg_ps[:, :], zeros[:, 0:P], zeros[:, :], start=False, stop=True).then_inc(agg_done, 1)

            def router(b):
                transposes(n_of(3, b))
                for k in range(KD):
                    last = pe.matmul(root_ps[:, 0:EX], hT[:, k, :], rw_sb[:, k, :], start=(k == 0), stop=(k == KD - 1))
                last.then_inc(logits, 1)

            def experts(b):
                def hidden(e):
                    pe.wait_ge(gelu_done, EX * b + e + 1)
                    for f in range(KD):
                        for k in range(KD):
                            last = pe.matmul(y_ps[e % 2][:, f * P:(f + 1) * P],
                                             w1_sb[:, e, k, f * P:(f + 1) * P], hT[:, k, :],
                                             start=(k == 0), stop=(k == KD - 1))
                    last.then_inc(hid_ready, 1)

                def second_product(e):
                    pe.wait_ge(gelu_done, 2 + EX * b + e + 1)
                    pe.wait_ge(acc_ready, (1 + EX) * b + 1 + max(e - 1, 0))
                    for f in range(KD):
                        last = pe.matmul(y_ps[2 + e % 2][:, 0:D], hidden_sb[e % 2][:, f, :], w2_sb[:, e, f, :],
                                         start=(f == 0), stop=(f == KD - 1))
                    last.then_inc(exp_ready, 1)

                hidden(0)
                hidden(1)
                for e in range(EX):
                    second_product(e)
                    if e + 2 < EX:
                        hidden(e + 2)
                    if e == 1:
                        pe.wait_ge(comb_ok, b + 1)
                        pe.transpose(comb_ps[0:EX, 0:P], comb[:, :], ident[:, :]).then_inc(combT_ps, 1)
                pe.wait_ge(combT_ok, b + 1)
                pe.matmul(root_ps[:, 0:D], combT[:, :], b2_sb[:, :], start=True, stop=True).then_inc(b2_ready, 1)

            for phase in range(4):
                if phase == 0:
                    pe.wait_ge(layer_w_in, 16 * 2 * KD)
                    transpose_h(0)
                    with pe.Fori(0, PAIRS) as i:
                        for q in range(2):
                            post_table0(2 * i + q, q)
                    for b in range(2 * PAIRS, BLOCKS):
                        post_table0(b, b % 2)
                    pe.wait_ge(weights_in, 16 * (3 + 2 * KD))
                    pe.transpose(comb_ps[:, 0:EX * KD], b1_rows[:, :], ident[0:EX * KD, 0:EX * KD]).then_inc(small_T, 1)
                    pe.wait_ge(root_taken, 1 + BLOCKS)
                    for k in range(KD):
                        last = pe.transpose(root_ps[:, k * EX:(k + 1) * EX], rw_rows[:, k * P:(k + 1) * P],
                                            ident[0:EX, 0:EX])
                    last.then_inc(small_T, 1)
                    pe.wait_ge(small_out, 2)
                    continue
                post = experts if phase == 3 else (lambda b, phase=phase: post_table(phase, b))
                sum_block(phase, 0)
                if phase < 3:
                    pe.wait_ge(layer_w_in, 16 * 2 * KD * (phase + 1))
                with pe.Fori(1, BLOCKS - 1) as b:
                    sum_block(phase, b, (lambda b=b: router(b - 1)) if phase == 3 else None)
                    post(b - 1)
                if phase == 3:
                    router(BLOCKS - 2)
                post(BLOCKS - 2)
                sum_block(phase, BLOCKS - 1)
                if phase == 3:
                    router(BLOCKS - 1)
                post(BLOCKS - 1)
                pe.matmul(agg_ps[:, :], zeros[:, 0:P], zeros[:, :], start=True, stop=True) \
                    .then_inc(tile_free, TILES_P - GROUP * (GROUPS - 1))


_INS = ["x", "src", "dst", "edge_type_8", "L0_gnn_weights", "L0_gnn_roots", "L0_gnn_biases", "L0_ffn_router_w",
        "L0_ffn_w1", "L0_ffn_b1", "L0_ffn_w2", "L0_ffn_b2"]


def kernel(**inputs):
    import numpy as _np
    import concourse.bacc as _bacc
    from concourse.bass_utils import run_bass_kernel_spmd as _run

    nc = _bacc.Bacc("TRN2", target_bir_lowering=False, num_devices=1)
    arrays, args = {}, []
    for name in _INS:
        a = _np.ascontiguousarray(inputs[name])
        arrays[f"in_{name}_dram"] = a
        args.append(nc.dram_tensor(f"in_{name}_dram", a.shape, mybir.dt.from_np(a.dtype), kind="ExternalInput").ap())
    out = nc.dram_tensor("out_dram", inputs["x"].shape, F32, kind="ExternalOutput").ap()
    gnn_moe(nc, *args, out)
    r = _run(nc, [arrays], core_ids=[0])
    return r.results[0]["out_dram"]
```
